# Optimizing a Trainium2 kernel written in Bass

```python
import numpy as np
import jax
import jax.numpy as jnp

def _softmax(x, axis=-1):
    return jax.nn.softmax(x, axis=axis)

def _gelu(x):
    return jax.nn.gelu(x, approximate=True)

def _silu(x):
    return jax.nn.silu(x)

def _sigmoid(x):
    return jax.nn.sigmoid(x)

def _layernorm(x, axis=-1, eps=1e-05):
    m = jnp.mean(x, axis=axis, keepdims=True)
    v = jnp.var(x, axis=axis, keepdims=True)
    return (x - m) / jnp.sqrt(v + eps)

def _scatter_add(tgt, idx, src, axis=0):
    return tgt.at[idx].add(src)

def _segment_sum(src, seg, n):
    return jax.ops.segment_sum(src, seg, n)
kernel_name = 'mk_adaln_ffn_d2_seqx_r2_8f540e'

def setup_inputs(seed: int=0):
    np.random.seed(seed)
    _w = jnp.asarray

    def _rec_inputs():
        import jax
        import jax.numpy as jnp
        _rk = jax.random.key(seed)
        x = -0.000125 + 0.9999 * jax.random.normal(jax.random.fold_in(_rk, 1), (4, 1024, 1024), jnp.float32)
        _lenS = 1024 - jax.random.randint(jax.random.fold_in(_rk, 7), (4,), 0, max(1, 1024 // 4) + 1, jnp.int32)
        _lenS2 = 1024 - jax.random.randint(jax.random.fold_in(_rk, 8), (4,), 0, max(1, 1024 // 4) + 1, jnp.int32)
        fside_BxSxS_0 = -1.52775e-05 + 0.999936 * jax.random.normal(jax.random.fold_in(_rk, 11), (4, 1024, 1024), jnp.float32)
        cond_512 = -5.03954e-05 + 1.00559 * jax.random.normal(jax.random.fold_in(_rk, 12), (4, 256), jnp.float32)
        return (x, fside_BxSxS_0, cond_512)
    x, fside_BxSxS_0, cond_512 = _rec_inputs()

    def _L0_cond_setup():
        import jax, jax.numpy as jnp
        from jax import lax
        import numpy as np
        B, T, C, TD = (8, 1024, 1024, 256)

        def _bi_wkv(r, k, v, w, u, time_emb):
            tf = jax.nn.sigmoid(jnp.sum(time_emb, axis=-1))[:, None, None]
            decay = jnp.exp(-jnp.exp(w.astype(jnp.float32)))[None, :] * (0.5 + 0.5 * tf[:, :, 0])
            kf = k.astype(jnp.float32)
            vf = v.astype(jnp.float32)
            ek = jnp.exp(jnp.minimum(kf, 30.0))
            ekv = ek * vf

            def step(carry, x):
                a, b = carry
                ekv_t, ek_t = x
                a = a * decay + ekv_t
                b = b * decay + ek_t
                return ((a, b), (a, b))
            ekv_t = jnp.swapaxes(ekv, 0, 1)
            ek_t = jnp.swapaxes(ek, 0, 1)
            init = (jnp.zeros_like(decay), jnp.zeros_like(decay))
            _, (nf, df) = lax.scan(step, init, (ekv_t, ek_t))
            _, (nb, db) = lax.scan(step, init, (ekv_t, ek_t), reverse=True)
            nf = jnp.swapaxes(nf, 0, 1)
            df = jnp.swapaxes(df, 0, 1)
            nb = jnp.swapaxes(nb, 0, 1)
            db = jnp.swapaxes(db, 0, 1)
            euk = jnp.exp(jnp.minimum(u.astype(jnp.float32)[None, None, :] + kf, 30.0))
            num = nf + nb - ekv + euk * vf
            den = df + db - ek + euk
            base = jax.nn.sigmoid(r.astype(jnp.float32)) * (num / jnp.maximum(den, 1e-08))
            out = base * (0.8 + 0.2 * tf)
            return out.astype(r.dtype)
        key = jax.random.key(seed)
        ks = jax.random.split(key, 6)
        return {'r': jax.random.normal(ks[0], (B, T, C), dtype=jnp.float32), 'k': jax.random.normal(ks[1], (B, T, C), dtype=jnp.float32), 'v': jax.random.normal(ks[2], (B, T, C), dtype=jnp.float32), 'w': jax.random.normal(ks[3], (C,), dtype=jnp.float32), 'u': jax.random.normal(ks[4], (C,), dtype=jnp.float32), 'time_emb': jax.random.normal(ks[5], (B, TD), dtype=jnp.float32)}
    _L0_cond_all = _L0_cond_setup()
    _L0_cond_in = {k: v for k, v in _L0_cond_all.items() if k in ('w', 'u')}
    del _L0_cond_all

    def _L0_ffn_setup():
        import jax, jax.numpy as jnp
        import numpy as np
        key = jax.random.key(seed)
        k1, k2, k3, k4 = jax.random.split(key, 4)
        B, S, D_IN, D_OUT = (4, 2048, 1024, 1024)
        x = jax.random.normal(k1, (B, S, D_IN), dtype=jnp.float32)
        weight = jax.random.normal(k2, (D_OUT, D_IN), dtype=jnp.float32) * 0.02
        scale_weight = jax.random.uniform(k3, (D_OUT,), dtype=jnp.float32, minval=0.5, maxval=1.5)
        bias = jax.random.normal(k4, (D_OUT,), dtype=jnp.float32) * 0.02
        return {'x': x, 'weight': weight, 'scale_weight': scale_weight, 'bias': bias}
    _L0_ffn_all = _L0_ffn_setup()
    _L0_ffn_in = {k: v for k, v in _L0_ffn_all.items() if k in ('weight', 'scale_weight', 'bias')}
    del _L0_ffn_all

    def _L1_cond_setup():
        import jax, jax.numpy as jnp
        from jax import lax
        import numpy as np
        B, T, C, TD = (8, 1024, 1024, 256)

        def _bi_wkv(r, k, v, w, u, time_emb):
            tf = jax.nn.sigmoid(jnp.sum(time_emb, axis=-1))[:, None, None]
            decay = jnp.exp(-jnp.exp(w.astype(jnp.float32)))[None, :] * (0.5 + 0.5 * tf[:, :, 0])
            kf = k.astype(jnp.float32)
            vf = v.astype(jnp.float32)
            ek = jnp.exp(jnp.minimum(kf, 30.0))
            ekv = ek * vf

            def step(carry, x):
                a, b = carry
                ekv_t, ek_t = x
                a = a * decay + ekv_t
                b = b * decay + ek_t
                return ((a, b), (a, b))
            ekv_t = jnp.swapaxes(ekv, 0, 1)
            ek_t = jnp.swapaxes(ek, 0, 1)
            init = (jnp.zeros_like(decay), jnp.zeros_like(decay))
            _, (nf, df) = lax.scan(step, init, (ekv_t, ek_t))
            _, (nb, db) = lax.scan(step, init, (ekv_t, ek_t), reverse=True)
            nf = jnp.swapaxes(nf, 0, 1)
            df = jnp.swapaxes(df, 0, 1)
            nb = jnp.swapaxes(nb, 0, 1)
            db = jnp.swapaxes(db, 0, 1)
            euk = jnp.exp(jnp.minimum(u.astype(jnp.float32)[None, None, :] + kf, 30.0))
            num = nf + nb - ekv + euk * vf
            den = df + db - ek + euk
            base = jax.nn.sigmoid(r.astype(jnp.float32)) * (num / jnp.maximum(den, 1e-08))
            out = base * (0.8 + 0.2 * tf)
            return out.astype(r.dtype)
        key = jax.random.key(seed)
        ks = jax.random.split(key, 6)
        return {'r': jax.random.normal(ks[0], (B, T, C), dtype=jnp.float32), 'k': jax.random.normal(ks[1], (B, T, C), dtype=jnp.float32), 'v': jax.random.normal(ks[2], (B, T, C), dtype=jnp.float32), 'w': jax.random.normal(ks[3], (C,), dtype=jnp.float32), 'u': jax.random.normal(ks[4], (C,), dtype=jnp.float32), 'time_emb': jax.random.normal(ks[5], (B, TD), dtype=jnp.float32)}
    _L1_cond_all = _L1_cond_setup()
    _L1_cond_in = {k: v for k, v in _L1_cond_all.items() if k in ('w', 'u')}
    del _L1_cond_all

    def _L1_ffn_setup():
        import jax, jax.numpy as jnp
        import numpy as np
        from jax import lax
        H = 1024
        I = 512
        E = 32
        K = 4
        SH_I = 1024
        EPS = 1e-06

        def _rmsnorm(x, w, eps=EPS):
            var = jnp.mean(jnp.square(x.astype(jnp.float32)), axis=-1, keepdims=True)
            return (x * lax.rsqrt(var + eps)).astype(x.dtype) * w
        key = jax.random.key(seed)
        ks = jax.random.split(key, 8)
        s = lambda d: 1.0 / np.sqrt(d)
        return {'x': jax.random.normal(ks[0], (2, 1024, H), jnp.float32), 'norm_w': jnp.ones((H,), jnp.float32), 'router_w': jax.random.normal(ks[1], (E, H), jnp.float32) * s(H), 'w1': jax.random.normal(ks[2], (E, H, 2 * I), jnp.float32) * s(H), 'w2': jax.random.normal(ks[3], (E, I, H), jnp.float32) * s(I), 'sg': jax.random.normal(ks[4], (H, SH_I), jnp.float32) * s(H), 'su': jax.random.normal(ks[5], (H, SH_I), jnp.float32) * s(H), 'sd': jax.random.normal(ks[6], (SH_I, H), jnp.float32) * s(SH_I)}
    _L1_ffn_all = _L1_ffn_setup()
    _L1_ffn_in = {k: v for k, v in _L1_ffn_all.items() if k in ('norm_w', 'router_w', 'w1', 'w2', 'sg', 'su', 'sd')}
    del _L1_ffn_all
    return {'x': x, 'fside_BxSxS_0': fside_BxSxS_0, 'cond_512': cond_512, 'L0_cond_w': _L0_cond_in['w'], 'L0_cond_u': _L0_cond_in['u'], 'L0_ffn_weight': _L0_ffn_in['weight'], 'L0_ffn_scale_weight': _L0_ffn_in['scale_weight'], 'L0_ffn_bias': _L0_ffn_in['bias'], 'L1_cond_w': _L1_cond_in['w'], 'L1_cond_u': _L1_cond_in['u'], 'L1_ffn_norm_w': _L1_ffn_in['norm_w'], 'L1_ffn_router_w': _L1_ffn_in['router_w'], 'L1_ffn_w1': _L1_ffn_in['w1'], 'L1_ffn_w2': _L1_ffn_in['w2'], 'L1_ffn_sg': _L1_ffn_in['sg'], 'L1_ffn_su': _L1_ffn_in['su'], 'L1_ffn_sd': _L1_ffn_in['sd']}

def reference(x, fside_BxSxS_0, cond_512, L0_cond_w, L0_cond_u, L0_ffn_weight, L0_ffn_scale_weight, L0_ffn_bias, L1_cond_w, L1_cond_u, L1_ffn_norm_w, L1_ffn_router_w, L1_ffn_w1, L1_ffn_w2, L1_ffn_sg, L1_ffn_su, L1_ffn_sd):
    import jax
    import jax.numpy as jnp

    def _L0_cond_ref(r, k, v, w, u, time_emb):
        import jax, jax.numpy as jnp
        from jax import lax
        import numpy as np
        B, T, C, TD = (8, 1024, 1024, 256)

        def _bi_wkv(r, k, v, w, u, time_emb):
            tf = jax.nn.sigmoid(jnp.sum(time_emb, axis=-1))[:, None, None]
            decay = jnp.exp(-jnp.exp(w.astype(jnp.float32)))[None, :] * (0.5 + 0.5 * tf[:, :, 0])
            kf = k.astype(jnp.float32)
            vf = v.astype(jnp.float32)
            ek = jnp.exp(jnp.minimum(kf, 30.0))
            ekv = ek * vf

            def step(carry, x):
                a, b = carry
                ekv_t, ek_t = x
                a = a * decay + ekv_t
                b = b * decay + ek_t
                return ((a, b), (a, b))
            ekv_t = jnp.swapaxes(ekv, 0, 1)
            ek_t = jnp.swapaxes(ek, 0, 1)
            init = (jnp.zeros_like(decay), jnp.zeros_like(decay))
            _, (nf, df) = lax.scan(step, init, (ekv_t, ek_t))
            _, (nb, db) = lax.scan(step, init, (ekv_t, ek_t), reverse=True)
            nf = jnp.swapaxes(nf, 0, 1)
            df = jnp.swapaxes(df, 0, 1)
            nb = jnp.swapaxes(nb, 0, 1)
            db = jnp.swapaxes(db, 0, 1)
            euk = jnp.exp(jnp.minimum(u.astype(jnp.float32)[None, None, :] + kf, 30.0))
            num = nf + nb - ekv + euk * vf
            den = df + db - ek + euk
            base = jax.nn.sigmoid(r.astype(jnp.float32)) * (num / jnp.maximum(den, 1e-08))
            out = base * (0.8 + 0.2 * tf)
            return out.astype(r.dtype)
        return _bi_wkv(r, k, v, w, u, time_emb)

    def _L0_ffn_ref(x, weight, scale_weight, bias):
        import jax, jax.numpy as jnp
        import numpy as np
        w = weight * scale_weight[:, None]
        out = jnp.einsum('bsi,oi->bso', x, w) + bias
        return out

    def _L1_cond_ref(r, k, v, w, u, time_emb):
        import jax, jax.numpy as jnp
        from jax import lax
        import numpy as np
        B, T, C, TD = (8, 1024, 1024, 256)

        def _bi_wkv(r, k, v, w, u, time_emb):
            tf = jax.nn.sigmoid(jnp.sum(time_emb, axis=-1))[:, None, None]
            decay = jnp.exp(-jnp.exp(w.astype(jnp.float32)))[None, :] * (0.5 + 0.5 * tf[:, :, 0])
            kf = k.astype(jnp.float32)
            vf = v.astype(jnp.float32)
            ek = jnp.exp(jnp.minimum(kf, 30.0))
            ekv = ek * vf

            def step(carry, x):
                a, b = carry
                ekv_t, ek_t = x
                a = a * decay + ekv_t
                b = b * decay + ek_t
                return ((a, b), (a, b))
            ekv_t = jnp.swapaxes(ekv, 0, 1)
            ek_t = jnp.swapaxes(ek, 0, 1)
            init = (jnp.zeros_like(decay), jnp.zeros_like(decay))
            _, (nf, df) = lax.scan(step, init, (ekv_t, ek_t))
            _, (nb, db) = lax.scan(step, init, (ekv_t, ek_t), reverse=True)
            nf = jnp.swapaxes(nf, 0, 1)
            df = jnp.swapaxes(df, 0, 1)
            nb = jnp.swapaxes(nb, 0, 1)
            db = jnp.swapaxes(db, 0, 1)
            euk = jnp.exp(jnp.minimum(u.astype(jnp.float32)[None, None, :] + kf, 30.0))
            num = nf + nb - ekv + euk * vf
            den = df + db - ek + euk
            base = jax.nn.sigmoid(r.astype(jnp.float32)) * (num / jnp.maximum(den, 1e-08))
            out = base * (0.8 + 0.2 * tf)
            return out.astype(r.dtype)
        return _bi_wkv(r, k, v, w, u, time_emb)

    def _L1_ffn_ref(x, norm_w, router_w, w1, w2, sg, su, sd):
        import jax, jax.numpy as jnp
        import numpy as np
        from jax import lax
        H = 1024
        I = 512
        E = 32
        K = 4
        SH_I = 1024
        EPS = 1e-06

        def _rmsnorm(x, w, eps=EPS):
            var = jnp.mean(jnp.square(x.astype(jnp.float32)), axis=-1, keepdims=True)
            return (x * lax.rsqrt(var + eps)).astype(x.dtype) * w
        B, S, _ = x.shape
        residual = x
        h = _rmsnorm(x, norm_w)
        flat = h.reshape(-1, H)
        T = flat.shape[0]
        logits = flat.astype(jnp.float32) @ router_w.T
        scores = jax.nn.softmax(logits, axis=-1)
        topk_w, topk_ids = lax.top_k(scores, K)
        topk_w = topk_w / jnp.sum(topk_w, axis=-1, keepdims=True)
        ids = topk_ids.reshape(-1)
        sort_idx = jnp.argsort(ids)
        tok_idx = sort_idx // K
        xs = jnp.take(flat, tok_idx, axis=0)
        group_sizes = jnp.bincount(ids, length=E).astype(jnp.int32)
        gu = lax.ragged_dot(xs, w1, group_sizes)
        g, u = jnp.split(gu, 2, axis=-1)
        act = jax.nn.silu(g) * u
        ys = lax.ragged_dot(act, w2, group_sizes)
        y = jnp.zeros((T * K, H), ys.dtype).at[sort_idx].set(ys)
        routed = jnp.sum(y.reshape(T, K, H) * topk_w[..., None].astype(ys.dtype), axis=1)
        shared = jax.nn.silu(flat @ sg) * (flat @ su) @ sd
        out = residual + (routed + shared).reshape(B, S, H)
        return out
    x = x + _L0_ffn_ref(_L0_cond_ref(x, fside_BxSxS_0, fside_BxSxS_0, L0_cond_w, L0_cond_u, cond_512), L0_ffn_weight, L0_ffn_scale_weight, L0_ffn_bias)
    x = x + _L1_ffn_ref(_L1_cond_ref(x, fside_BxSxS_0, fside_BxSxS_0, L1_cond_w, L1_cond_u, cond_512), L1_ffn_norm_w, L1_ffn_router_w, L1_ffn_w1, L1_ffn_w2, L1_ffn_sg, L1_ffn_su, L1_ffn_sd)
    return x

_drawn_inputs = setup_inputs


def setup_inputs(seed=0):
    import zlib

    import numpy as np

    out = dict(_drawn_inputs(seed))
    spreads = {'L1_ffn_norm_w': (1.0, 0.2)}
    factors = {}
    for name, (base, spread) in spreads.items():
        noise = np.random.default_rng([zlib.crc32(name.encode()), seed]).standard_normal(out[name].shape)
        drawn = base * np.exp(spread * noise) if base else spread * noise
        out[name] = jnp.asarray(drawn.astype(out[name].dtype))
    for name, factor in factors.items():
        out[name] = (out[name] * factor).astype(out[name].dtype)
    return out
```

```python
import concourse.bass as bass
from concourse import mybir
from contextlib import ExitStack
import numpy as np

BATCH, SEQ, CH, COND = 4, 1024, 1024, 256
EXPERTS, TOPK, INNER = 32, 4, 512
SHARED = 2
P = 128
CB = CH // P
TOK = BATCH * SEQ
TT = TOK // P
ST = SEQ // P
ROUTED_TILES = TOK * TOPK // P + EXPERTS
SLOT_TILES = ROUTED_TILES + 2
SHARED_TILES = SHARED * TT
FILLS = 2
GROUPS = 6
GC = CB * 2 * INNER // 4
BLOCKS = BATCH * CB


def adaln_moe(nc, x_t, side_t, cond, w_u, lin_w, lin_sb, norm_w, router_t, expert_w, out):
    f32, f32r, bf16 = mybir.dt.float32, mybir.dt.float32r, mybir.dt.bfloat16
    i32, u32 = mybir.dt.int32, mybir.dt.uint32
    ALU, ACT, AX = mybir.AluOpType, mybir.ActivationFunctionType, mybir.AxisListType
    ds = bass.ds

    ratio_dram = nc.dram_tensor("ratio_dram", (BLOCKS * P, SEQ), f32).ap()
    rows_dram = nc.dram_tensor("rows_dram", (TOK + P, CH), f32).ap()
    slots_dram = nc.dram_tensor("slots_dram", (SLOT_TILES * P, 4), i32).ap()

    ctx = ExitStack()
    with ctx:
        def sb(name, cols, dt=f32):
            return ctx.enter_context(nc.sbuf_tensor(name, [P, cols], dt))

        def sem(name):
            return ctx.enter_context(nc.semaphore(name))

        halves = sb("halves", 34 * 1024, f32r)
        PAR = CB * SEQ
        C0HI, C0LO, W0HI, W0LO = 0, 2 * PAR, 4 * PAR, 4 * PAR + 1024
        EW = GROUPS * GC
        whi, wlo = halves[:, 0:EW], halves[:, EW:2 * EW]
        xhi, xlo = halves[:, 2 * EW:2 * EW + 1024], halves[:, 2 * EW + 1024:2 * EW + 2048]
        ahi, alo = halves[:, 2 * EW + 2048:2 * EW + 2560], halves[:, 2 * EW + 2560:2 * EW + 3072]
        w0hi, w0lo = halves[:, W0HI:W0HI + 1024], halves[:, W0LO:W0LO + 1024]

        WORK = EW + 2560 + 4 * SLOT_TILES + 2 * (SHARED_TILES + SLOT_TILES)
        work = sb("work", WORK)
        (K, X, EK, EKV, W, F, G, H, N, WST, XL, C1, RL, RS, ZS) = (
            work[:, i * 1024:(i + 1) * 1024] for i in range(15))
        stage = work[:, 0:EW]
        hx = work[:, EW:EW + 1024]
        y = work[:, EW + 1024:EW + 2048]
        act = work[:, EW + 2048:EW + 2560]
        slots = work[:, EW + 2560:EW + 2560 + 4 * SLOT_TILES].bitcast(i32)
        GT = SHARED_TILES + SLOT_TILES
        gains = work[:, WORK - 2 * GT:WORK]

        LG, CAND, RESET, CNT, INCL = X, EK, XL, C1, H
        HOT = [EKV, W, F, G]
        chosen = N[:, 0:512].bitcast(bf16)
        rms, small, rampf, rev, ramp128, ends = (WST[:, i * 32:(i + 1) * 32] for i in range(6))
        tops = WST[:, 256:256 + TOPK * TT]
        EXP30 = float(np.exp(np.float32(30.0)))

        acc = sb("acc", TT * 33)
        decay = sb("decay", 2 * BLOCKS)
        uu = sb("uu", 2 * CB)
        ww = sb("ww", 2 * CB)
        lsb = sb("lsb", 2 * CB)
        nrm = sb("nrm", CB)
        rw = sb("rw", CB * EXPERTS)
        ident = sb("ident", P)
        ones = sb("ones", 1)
        before = sb("before", P, bf16)
        allb = sb("allb", P, bf16)
        tf = sb("tf", BATCH)
        half_tf = sb("half_tf", BATCH)
        neg_gain = sb("neg_gain", BATCH)
        entry = sb("entry", TT * TOPK * 4, i32)
        where = sb("where", TT * TOPK, i32)
        bounds = sb("bounds", EXPERTS + 1, i32)
        row_idx = sb("row_idx", 1, i32)
        add_idx = sb("add_idx", 1, i32)
        ramp = where[:, 0:EXPERTS]
        put_idx = sb("put_idx", TOPK, i32)
        put_val = sb("put_val", TOPK * 4, i32)

        ps = [ctx.enter_context(nc.psum_tensor(f"ps{i}", [P, 1024], f32)) for i in range(4)]
        ps_x1, ps_z, ps_r, ps_l = ps
        ps_h, ps_xt, ps_y = ps[0], ps[1], ps[2]
        ps_at = [ps[3][:, 0:256], ps[3][:, 512:768]]

        s = {}
        for name in (
            "k_in x_in ramp w0_in xl_in rl_in consts_in cond_in kc ek ekv euk w_diff h_fwd h_bwd h_sum h_all den "
            "g_ln g_inv nf nb n_sum wv_done num newton1 newton2 sig_x gated gated_hi gated_lo ratio ratio_out "
            "w0_hi w0_lo ffn_done x1_pre sig_x1 c1 res sq z r_tr z_tr l_mm r_copy z_copy r_out z_out l_acc "
            "prep prep_act masks rt rt_act rt_mask rt_pe fill_set add_idx_set gated_raw apart entry_ready put_set put_out "
            "slots_in gains_set w_hi w_lo w1_read w2_read rows_in row_idx_set x_tr x_hi x_lo h_mm "
            "silu_done act_done a_tr a_hi a_lo y_mm y_hi y_lo y_out zero_set zero_out"
        ).split():
            s[name] = sem(name)

        ONE_AHEAD = (
            "wv_done gated w0_lo r_tr l_mm ratio_out w_lo ffn_done num z_tr r_out z_out a_tr "
            "w1_read w2_read x1_pre r_copy z_copy l_acc act_done x_lo y_lo y_hi"
        ).split()
        w_in = [sem(f"w_in{q}") for q in range(GROUPS)]
        block = ctx.enter_context(nc.Block())

        def apart(eng):
            eng.sem_inc(s["apart"], 1)

        def shared_loop(eng, weights, tile):
            with eng.Fori(0, SHARED) as j:
                weights(j, j * TT)
                with eng.Fori(j * TT, j * TT + TT) as g:
                    tile(g, j)

        def routed_loop(eng, weights, tile):
            with eng.Fori(0, EXPERTS) as e:
                first = eng.value_load(bounds[0:1, ds(e, 1)], min_val=0, max_val=ROUTED_TILES)
                last = eng.value_load(bounds[0:1, ds(e + 1, 1)], min_val=1, max_val=ROUTED_TILES)
                weights(e + SHARED, first + SHARED_TILES)
                with eng.Fori(first + SHARED_TILES, last + SHARED_TILES) as g:
                    tile(g, e + SHARED)

        @block.sync
        def _(sp):
            for name in ONE_AHEAD:
                sp.sem_inc(s[name], 1)
            sp.dma_start(ww[:, :], w_u[0]).then_inc(s["cond_in"], 16)
            sp.dma_start(work[:, 0:BATCH * COND], cond.to_broadcast([P, BATCH * COND])).then_inc(s["cond_in"], 16)
            for dst, src in ((uu, w_u[1]), (lsb, lin_sb), (nrm, norm_w), (rw, router_t)):
                sp.dma_start(dst[:, :], src).then_inc(s["consts_in"], 16)
            sp.wait_ge(s["prep"], 1)

            def load_unit(u):
                sp.wait_ge(s["wv_done"], 2 * u + 1)
                sp.dma_start(K, side_t[ds(u * P, P), :]).then_inc(s["k_in"], 16)
                sp.wait_ge(s["gated"], u + 1)
                sp.dma_start(X, x_t[ds(u * P, P), :]).then_inc(s["x_in"], 16)

            def load_linear(v, o):
                sp.wait_ge(s["w0_lo"], v + 1)
                sp.dma_start(WST, lin_w[ds(o * P, P), :]).then_inc(s["w0_in"], 16)
                sp.wait_ge(s["r_tr"], v + 1)
                sp.dma_start(XL, x_t[ds(v * P, P), :]).then_inc(s["xl_in"], 16)
                sp.wait_ge(s["l_mm"], v + 1)
                sp.dma_start(RL, ratio_dram[ds(v * P, P), :]).then_inc(s["rl_in"], 16)

            def store_ratio(u):
                sp.wait_ge(s["ratio"], u + 1)
                sp.dma_start(ratio_dram[ds(u * P, P), :], N).then_inc(s["ratio_out"], 16)

            def store_rows(v, b, o):
                rows = out[ds(b * SEQ, SEQ), ds(o * P, P)].rearrange("(t p) c -> p t c", p=P)
                sp.wait_ge(s["r_copy"], v + 2)
                sp.dma_start(rows, RS.rearrange("p (t c) -> p t c", c=P)).then_inc(s["r_out"], 16)
                rows = rows_dram[ds(b * SEQ, SEQ), ds(o * P, P)].rearrange("(t p) c -> p t c", p=P)
                sp.wait_ge(s["z_copy"], v + 2)
                sp.dma_start(rows, ZS.rearrange("p (t c) -> p t c", c=P)).then_inc(s["z_out"], 16)

            with sp.Fori(0, CB) as c:
                load_unit(c)
                store_ratio(c)
            with sp.Fori(1, BATCH) as b:
                with sp.Fori(0, CB) as c:
                    sp.wait_ge(s["ratio_out"], 16 * (b * CB + c) + 1)
                    load_linear((b - 1) * CB + c, c)
                    load_unit(b * CB + c)
                    store_ratio(b * CB + c)
                    store_rows((b - 1) * CB + c, b - 1, c)
            sp.wait_ge(s["ratio_out"], 16 * BLOCKS + 1)
            with sp.Fori(0, CB) as c:
                load_linear((BATCH - 1) * CB + c, c)
                store_rows((BATCH - 1) * CB + c, BATCH - 1, c)

            sp.wait_ge(s["zero_set"], 1)
            sp.dma_start(rows_dram[TOK:TOK + P, :], K).then_inc(s["zero_out"], 16)
            sp.wait_ge(s["zero_out"], 16)
            sp.wait_ge(s["y_out"], 16)
            sp.wait_ge(s["entry_ready"], 1)

            def weights(j, g):
                for q in range(GROUPS):
                    sp.wait_ge(s["w_lo"], GROUPS * j + 1)
                    sp.dma_start(stage[:, q * GC:(q + 1) * GC],
                                 expert_w[ds((j * GROUPS + q) * P, P), :]).then_inc(w_in[q], 16)

            with sp.Fori(0, SHARED) as j:
                weights(j, None)
            sp.wait_ge(s["put_out"], 16 * (TT * TOPK + FILLS))
            sp.dma_start(slots.rearrange("p (t w) -> p t w", w=4),
                         slots_dram.rearrange("(t p) w -> p t w", p=P)).then_inc(s["slots_in"], 16)
            with sp.Fori(SHARED, SHARED + EXPERTS) as j:
                weights(j, None)

        @block.gpsimd
        def _(pool):
            pool.memset(ident[:, :], 0.0).then_inc(s["masks"], 1)
            pool.memset(allb[:, :], 1.0).then_inc(s["masks"], 1)
            pool.memset(before[:, :], 1.0).then_inc(s["masks"], 1)
            pool.memset(ones[:, :], 1.0).then_inc(s["masks"], 1)
            pool.memset(acc[:, :], 0.0).then_inc(s["masks"], 1)
            pool.wait_ge(s["masks"], 5)
            pool.affine_select(out=ident[:, :], in_=ident[:, :], compare_op=ALU.not_equal, fill=1.0,
                               base=0, pattern=[[-1, P]], channel_multiplier=1).then_inc(s["masks"], 1)
            pool.affine_select(out=before[:, :], in_=before[:, :], compare_op=ALU.is_gt, fill=0.0,
                               base=0, pattern=[[1, P]], channel_multiplier=-1).then_inc(s["masks"], 1)


            pool.iota(ramp, pattern=[[1, EXPERTS]], base=0, channel_multiplier=0).then_inc(s["ramp"], 1)
            pool.iota(entry[:, :].rearrange("p (t k w) -> p t k w", k=TOPK, w=4)[:, :, :, 0],
                      pattern=[[P, TT], [0, TOPK]], base=0, channel_multiplier=1).then_inc(s["ramp"], 1)
            pool.wait_ge(s["z_out"], 16 * BLOCKS + 1)
            pool.wait_ge(s["r_out"], 16 * BLOCKS + 1)
            pool.memset(slots, 0).then_inc(s["fill_set"], 1)
            pool.wait_ge(s["fill_set"], 1)
            pool.iota(slots.rearrange("p (t w) -> p t w", w=4)[:, :, 0], pattern=[[0, SLOT_TILES]],
                      base=TOK, channel_multiplier=1).then_inc(s["fill_set"], 1)
            pool.wait_ge(s["fill_set"], 2)
            for t in range(0, SLOT_TILES, SLOT_TILES // FILLS):
                n = SLOT_TILES // FILLS
                pool.dma_start(slots_dram[t * P:(t + n) * P, :].rearrange("(t p) w -> p t w", p=P),
                               slots[:, 4 * t:4 * (t + n)].rearrange("p (t w) -> p t w", w=4)).then_inc(s["put_out"], 16)
            pool.wait_ge(s["zero_set"], 1)
            pool.dma_start(out[TOK:TOK + P, :], K).then_inc(s["y_out"], 16)

            def load_rows(t):
                pool.dma_start(hx, rows_dram[ds(t * P, P), :]).then_inc(s["rows_in"], 16)

            def gather_rows(g):
                pool.tensor_copy(row_idx[:, :], slots[:, ds((g - SHARED_TILES) * 4, 1)]).then_inc(s["row_idx_set"], 1)
                pool.wait_ge(s["row_idx_set"], g - (SHARED_TILES - 1))
                apart(pool)
                pool.indirect_dma_start(hx, None, rows_dram[:, :],
                                        bass.IndirectOffsetOnAxis(row_idx[:, :].bitcast(u32), 0)).then_inc(s["rows_in"], 16)

            def await_y(g):
                pool.wait_ge(s["y_hi"], g + 2)
                pool.wait_ge(s["y_lo"], g + 2)
                pool.wait_ge(s["y_out"], 16 * (g + 1))

            def add_rows(g, t):
                await_y(g)
                pool.dma_start(out[ds(t * P, P), :], y, accum_op=ALU.add).then_inc(s["y_out"], 16)

            def put_entries(t):
                pool.wait_ge(s["put_out"], 16 * (TOPK * t + FILLS))
                pool.tensor_copy(put_idx[:, :], where[:, ds(t * TOPK, TOPK)]).then_inc(s["put_set"], 1)
                pool.tensor_copy(put_val[:, :], entry[:, ds(t * TOPK * 4, TOPK * 4)]).then_inc(s["put_set"], 1)
                pool.wait_ge(s["put_set"], 2 * t + 2)
                for k in range(TOPK):
                    apart(pool)
                    pool.indirect_dma_start(slots_dram[:, :], bass.IndirectOffsetOnAxis(put_idx[:, k:k + 1].bitcast(u32), 0),
                                            put_val[:, 4 * k:4 * k + 4], None).then_inc(s["put_out"], 16)

            pool.wait_ge(s["zero_out"], 16)
            pool.wait_ge(s["entry_ready"], 1)
            load_rows(0)
            pool.wait_ge(s["x_tr"], 1)
            load_rows(1)
            with pool.Fori(0, TT) as g:
                put_entries(g)
                pool.wait_ge(s["x_tr"], g + 2)
                load_rows((g + 2) % TT)
                add_rows(g, g)
            with pool.Fori(0, TT - 2) as t:
                pool.wait_ge(s["x_tr"], t + (TT + 2))
                load_rows(t + 2)
                add_rows(t + TT, t)
            pool.wait_ge(s["slots_in"], 16)
            for g in range(SHARED_TILES - 2, SHARED_TILES):
                pool.wait_ge(s["x_tr"], g + 2)
                gather_rows(g + 2)
                add_rows(g, g - TT)
            tiles = pool.value_load(bounds[0:1, EXPERTS:EXPERTS + 1], min_val=EXPERTS, max_val=ROUTED_TILES)
            with pool.Fori(SHARED_TILES, tiles + SHARED_TILES) as g:
                pool.wait_ge(s["x_tr"], g + 2)
                gather_rows(g + 2)
                await_y(g)
                pool.tensor_copy(add_idx[:, :], slots[:, ds((g - SHARED_TILES) * 4, 1)]).then_inc(s["add_idx_set"], 1)
                pool.wait_ge(s["add_idx_set"], g - (SHARED_TILES - 1))
                apart(pool)
                pool.indirect_dma_start(out[:, :], bass.IndirectOffsetOnAxis(add_idx[:, :].bitcast(u32), 0),
                                        y, None, compute_op=ALU.add).then_inc(s["y_out"], 16)
            pool.wait_ge(s["rows_in"], (tiles + (SHARED_TILES + 2)) * 16)
            pool.wait_ge(s["y_out"], (tiles + (SHARED_TILES + 1)) * 16)

        @block.scalar
        def _(sc):
            sc.wait_ge(s["prep"], 1)
            sc.activation(tf[:, :], tf[:, :], ACT.Sigmoid).then_inc(s["prep_act"], 1)
            sc.wait_ge(s["cond_in"], 32)
            sc.activation(ww[:, :], ww[:, :], ACT.Exp).then_inc(s["prep_act"], 1)
            sc.wait_ge(s["prep_act"], 2)
            sc.activation(ww[:, :], ww[:, :], ACT.Exp, scale=-1.0).then_inc(s["prep_act"], 1)

            def split_linear(v):
                sc.wait_ge(s["w0_in"], (v + 1) * 16)
                sc.wait_ge(s["ffn_done"], v + 1)
                sc.activation(w0hi, WST, ACT.Copy).then_inc(s["w0_hi"], 1)

            def unit(u, c, par, freed):
                sc.wait_ge(s["kc"], u + 1)
                sc.activation(EK, EK, ACT.Exp).then_inc(s["ek"], 1)

                def euk(l):
                    sc.wait_ge(s["num"], u * 2 + l + 1)
                    apart(sc)
                    sc.activation(W, K, ACT.Exp, bias=uu[:, ds(c + l * CB, 1)]).then_inc(s["euk"], 1)

                def inverse(l):
                    sc.wait_ge(s["den"], u * 2 + l + 1)
                    sc.activation(G, H, ACT.Ln).then_inc(s["g_ln"], 1)
                    sc.wait_ge(s["g_ln"], u * 2 + l + 1)
                    sc.activation(G, G, ACT.Exp, scale=-1.0).then_inc(s["g_inv"], 1)

                euk(0)
                sc.wait_ge(s["x_in"], (u + 1) * 16)
                sc.activation(X, X, ACT.Sigmoid).then_inc(s["sig_x"], 1)
                inverse(0)
                euk(1)
                sc.wait_ge(s["gated"], u + 2)
                if freed is not None:
                    sc.wait_ge(s["ffn_done"], freed + 1)
                apart(sc)
                sc.activation(halves[:, ds(c * SEQ + par * PAR + C0HI, SEQ)], N, ACT.Copy).then_inc(s["gated_hi"], 1)
                inverse(1)

            def linear(v, o):
                sc.wait_ge(s["x1_pre"], v + 2)
                sc.wait_ge(s["z_tr"], v + 1)
                sc.wait_ge(s["l_mm"], v + 1)
                apart(sc)
                sc.activation(C1, XL, ACT.Sigmoid, bias=lsb[:, ds(o + CB, 1)]).then_inc(s["sig_x1"], 1)
                sc.wait_ge(s["c1"], v + 1)
                sc.activation(RL, C1, ACT.Square).then_inc(s["sq"], 1)
                sc.wait_ge(s["r_tr"], v + 2)
                sc.wait_ge(s["r_out"], v * 16 + 1)
                sc.activation(RS, ps_r[:, :], ACT.Copy).then_inc(s["r_copy"], 1)
                sc.wait_ge(s["z_tr"], v + 2)
                sc.wait_ge(s["z_out"], v * 16 + 1)
                sc.activation(ZS, ps_z[:, :], ACT.Copy).then_inc(s["z_copy"], 1)

            sc.wait_ge(s["consts_in"], 64)
            with sc.Fori(0, CB) as c:
                unit(c, c, 0, None)
            with sc.Fori(1, BATCH) as b:
                with sc.Fori(0, CB) as c:
                    split_linear(b * CB + c - CB)
                    unit(b * CB + c, c, b % 2, b * CB - CB)
                    linear(b * CB + c - CB, c)
            with sc.Fori(0, CB) as c:
                split_linear(c + (BATCH - 1) * CB)
                linear(c + (BATCH - 1) * CB, c)

            sc.wait_ge(s["rt_mask"], 1)
            sc.activation(rms, rms, ACT.Sqrt).then_inc(s["rt_act"], 1)
            sc.wait_ge(s["rt_mask"], 2)
            sc.activation(tops, tops, ACT.Exp).then_inc(s["rt_act"], 1)

            def split_x(g):
                sc.wait_ge(s["x_tr"], g + 1)
                sc.activation(xhi, ps_xt[:, :], ACT.Copy).then_inc(s["x_hi"], 1)

            def weights(j, g):
                for q in range(GROUPS):
                    sc.wait_ge(w_in[q], (j + 1) * 16)
                    sc.wait_ge(s["w1_read"] if q < 4 else s["w2_read"], g * (4 if q < 4 else 2) + 1)
                    sc.activation(whi[:, q * GC:(q + 1) * GC], stage[:, q * GC:(q + 1) * GC],
                                  ACT.Copy).then_inc(s["w_hi"], 1)

            def tile(g, j):
                for a in range(2):
                    sc.wait_ge(s["w1_read"], g * 4 + 2 * a + 3)
                    sc.wait_ge(s["a_tr"], g * 2 + 1)
                    apart(sc)
                    sc.activation(act[:, a * 256:a * 256 + 256], ps_h[:, a * 512:a * 512 + 256], ACT.Silu,
                                  scale=gains[:, ds(g + GT, 1)]).then_inc(s["silu_done"], 1)
                for a in range(2):
                    sc.wait_ge(s["a_tr"], g * 2 + a + 2)
                    sc.wait_ge(s["w2_read"], g * 2 + 1)
                    sc.activation(ahi[:, a * 256:a * 256 + 256], ps_at[a],
                                  ACT.Copy).then_inc(s["a_hi"], 1)
                split_x(g + 1)
                sc.wait_ge(s["w2_read"], g * 2 + 3)
                sc.wait_ge(s["y_out"], (g + 1) * 16)
                apart(sc)
                sc.activation(y[:, 0:512], ps_y[:, 0:512], ACT.Copy, scale=gains[:, ds(g, 1)]).then_inc(s["y_hi"], 1)

            split_x(0)
            shared_loop(sc, weights, tile)
            sc.wait_ge(s["gains_set"], 2)
            routed_loop(sc, weights, tile)

        @block.vector
        def _(ve):
            ve.wait_ge(s["cond_in"], 32)
            ve.reduce_sum(tf[:, :], work[:, 0:BATCH * COND].rearrange("p (b d) -> p b d", b=BATCH),
                          axis=AX.X).then_inc(s["prep"], 1)
            ve.wait_ge(s["prep_act"], 3)
            ve.tensor_scalar(half_tf[:, :], tf[:, :], 0.5, 0.5, ALU.mult, ALU.add).then_inc(s["prep"], 1)
            ve.tensor_scalar(neg_gain[:, :], tf[:, :], -0.2, -0.8, ALU.mult, ALU.add).then_inc(s["prep"], 1)
            ve.wait_ge(s["prep"], 3)
            for l in range(2):
                for b in range(BATCH):
                    ve.tensor_scalar(decay[:, l * BLOCKS + b * CB:l * BLOCKS + (b + 1) * CB], ww[:, l * CB:(l + 1) * CB],
                                     half_tf[:, b:b + 1], None, ALU.mult).then_inc(s["prep"], 1)
            ve.wait_ge(s["prep"], 3 + 2 * BATCH)
            ve.wait_ge(s["consts_in"], 64)

            def split_linear(v):
                ve.wait_ge(s["w0_hi"], v + 1)
                ve.tensor_tensor(w0lo, WST, w0hi.bitcast(f32), ALU.subtract).then_inc(s["w0_lo"], 1)

            def unit(u, b, c, par):
                ve.wait_ge(s["k_in"], (u + 1) * 16)
                ve.tensor_scalar(EK, K, 30.0, None, ALU.min).then_inc(s["kc"], 1)
                ve.wait_ge(s["ek"], u + 1)
                ve.tensor_tensor(EKV, EK, K, ALU.mult).then_inc(s["ekv"], 1)
                for l in range(2):
                    n = u * 2 + l
                    d = decay[:, ds(u + l * BLOCKS, 1)].to_broadcast([P, SEQ])
                    ve.tensor_tensor_scan(H, d, EK, 0.0, ALU.mult, ALU.add).then_inc(s["h_fwd"], 1)
                    ve.tensor_tensor_scan(G[:, ::-1], d, EK[:, ::-1], 0.0, ALU.mult, ALU.add).then_inc(s["h_bwd"], 1)
                    ve.wait_ge(s["euk"], n + 1)
                    ve.scalar_tensor_tensor(W, W, EXP30, EK, ALU.min, ALU.subtract).then_inc(s["w_diff"], 1)
                    if l == 0:
                        ve.wait_ge(s["ekv"], u + 1)
                    ve.tensor_tensor_scan(F, d, EKV, 0.0, ALU.mult, ALU.add).then_inc(s["nf"], 1)
                    ve.wait_ge(s["h_bwd"], n + 1)
                    ve.wait_ge(s["h_fwd"], n + 1)
                    ve.tensor_tensor(H, H, G, ALU.add).then_inc(s["h_sum"], 1)
                    if l == 0:
                        ve.wait_ge(s["ratio_out"], u * 16 + 1)
                    else:
                        ve.wait_ge(s["gated_hi"], u + 1)
                        ve.tensor_tensor(halves[:, ds(c * SEQ + par * PAR + C0LO, SEQ)], N,
                                         halves[:, ds(c * SEQ + par * PAR + C0HI, SEQ)].bitcast(f32),
                                         ALU.subtract).then_inc(s["gated_lo"], 1)
                        ve.wait_ge(s["gated_lo"], u + 1)
                    ve.tensor_tensor_scan(N[:, ::-1], d, EKV[:, ::-1], 0.0, ALU.mult, ALU.add).then_inc(s["nb"], 1)
                    ve.wait_ge(s["h_sum"], n + 1)
                    ve.wait_ge(s["w_diff"], n + 1)
                    ve.tensor_tensor(H, H, W, ALU.add).then_inc(s["h_all"], 1)
                    ve.wait_ge(s["nf"], n + 1)
                    ve.wait_ge(s["nb"], n + 1)
                    ve.tensor_tensor(F, F, N, ALU.add).then_inc(s["n_sum"], 1)
                    ve.wait_ge(s["h_all"], n + 1)
                    ve.tensor_scalar(H, H, 1e-8, None, ALU.max).then_inc(s["den"], 1)
                    ve.tensor_tensor(W, W, K, ALU.mult).then_inc(s["wv_done"], 1)
                    ve.wait_ge(s["n_sum"], n + 1)
                    ve.wait_ge(s["wv_done"], n + 2)
                    ve.tensor_tensor(F, F, W, ALU.add).then_inc(s["num"], 1)
                    ve.wait_ge(s["g_inv"], n + 1)
                    ve.wait_ge(s["den"], n + 1)
                    ve.tensor_tensor(N, H, G, ALU.mult).then_inc(s["newton1"], 1)
                    ve.wait_ge(s["newton1"], n + 1)
                    ve.scalar_tensor_tensor(N, N, 2.0, G, ALU.subtract, ALU.mult).then_inc(s["newton2"], 1)
                    ve.wait_ge(s["newton2"], n + 1)
                    ve.wait_ge(s["num"], n + 2)
                    ve.scalar_tensor_tensor(N, F, neg_gain[:, ds(b, 1)] if not isinstance(b, int) else neg_gain[:, b:b + 1],
                                            N, ALU.mult, ALU.mult).then_inc(s["gated_raw"] if l == 0 else s["ratio"], 1)
                    if l == 0:
                        ve.wait_ge(s["gated_raw"], u + 1)
                        ve.wait_ge(s["sig_x"], u + 1)
                        ve.tensor_tensor(N, N, X, ALU.mult).then_inc(s["gated"], 1)

            def linear(v, b, o):
                ve.wait_ge(s["ffn_done"], v + 2)
                ve.wait_ge(s["xl_in"], (v + 1) * 16)
                ve.scalar_tensor_tensor(XL, ps_x1[:, :], lsb[:, ds(o, 1)], XL, ALU.mult, ALU.add).then_inc(s["x1_pre"], 1)
                ve.wait_ge(s["sig_x1"], v + 1)
                ve.wait_ge(s["rl_in"], (v + 1) * 16)
                ve.tensor_tensor(C1, C1, RL, ALU.mult).then_inc(s["c1"], 1)
                ve.wait_ge(s["c1"], v + 1)
                ve.scalar_tensor_tensor(XL, XL, lsb[:, ds(o + CB, 1)], C1, ALU.add, ALU.add).then_inc(s["res"], 1)
                ve.wait_ge(s["sq"], v + 1)
                ve.tensor_scalar(C1, C1, nrm[:, ds(o, 1)], None, ALU.mult).then_inc(s["z"], 1)
                ve.wait_ge(s["l_mm"], v + 2)
                part = acc[:, ds(b * (ST * 33), ST * 33)]
                ve.wait_ge(s["l_acc"], v + 1)
                ve.tensor_tensor(part, ps_l[:, 0:ST * 33], part, ALU.add).then_inc(s["l_acc"], 1)

            ve.wait_ge(s["masks"], 5)
            with ve.Fori(0, CB) as c:
                unit(c, 0, c, 0)
            with ve.Fori(1, BATCH) as b:
                with ve.Fori(0, CB) as c:
                    split_linear(b * CB + c - CB)
                    unit(b * CB + c, b, c, b % 2)
                    linear(b * CB + c - CB, b - 1, c)
            with ve.Fori(0, CB) as c:
                split_linear(c + (BATCH - 1) * CB)
                linear(c + (BATCH - 1) * CB, BATCH - 1, c)

            ve.wait_ge(s["ratio_out"], 16 * BLOCKS + 1)
            ve.memset(K, 0.0).then_inc(s["zero_set"], 1)
            ve.wait_ge(s["ramp"], 2)
            ve.wait_ge(s["r_tr"], BLOCKS + 1)
            ve.wait_ge(s["z_tr"], BLOCKS + 1)
            steps = [0]

            def done(instruction):
                steps[0] += 1
                instruction.then_inc(s["rt"], 1)
                ve.wait_ge(s["rt"], steps[0])

            te = lambda a: a.rearrange("p (t e) -> p t e", e=EXPERTS)
            per_t = lambda a: a.rearrange("p (t o) -> p t o", o=1).to_broadcast([P, TT, EXPERTS])
            per_e = lambda a: a.rearrange("p (o e) -> p o e", o=1).to_broadcast([P, TT, EXPERTS])
            acc3 = acc[:, :].rearrange("p (t e) -> p t e", e=EXPERTS + 1)
            ve.wait_ge(s["l_acc"], BLOCKS + 1)
            done(ve.tensor_copy(rampf, ramp))
            done(ve.tensor_scalar(rev, rampf, -1.0, float(EXPERTS), ALU.mult, ALU.add))
            done(ve.tensor_scalar(ramp128, rampf, float(P), None, ALU.mult))
            ve.tensor_scalar(rms, acc3[:, :, EXPERTS], 1.0 / CH, 1e-6, ALU.mult, ALU.add).then_inc(s["rt_mask"], 1)
            ve.wait_ge(s["rt_act"], 1)
            done(ve.reciprocal(rms, rms))
            done(ve.tensor_tensor(te(LG), acc3[:, :, 0:EXPERTS], per_t(rms), ALU.mult))
            for k in range(TOPK):
                top = tops[:, k * TT:(k + 1) * TT]
                done(ve.reduce_max(top, te(LG), axis=AX.X))
                done(ve.tensor_tensor(te(CAND), te(LG), per_t(top), ALU.is_equal))
                done(ve.tensor_tensor(te(CAND), te(CAND), per_e(rev), ALU.mult))
                done(ve.reduce_max(small, te(CAND), axis=AX.X))
                done(ve.tensor_tensor(te(HOT[k]), te(CAND), per_t(small), ALU.is_equal))
                done(ve.scalar_tensor_tensor(LG, HOT[k], -1e30, LG, ALU.mult, ALU.add))
            tops3 = tops.rearrange("p (k t) -> p k t", k=TOPK)
            first = tops[:, 0:TT].rearrange("p (o t) -> p o t", o=1).to_broadcast([P, TOPK, TT])
            done(ve.tensor_copy(small, tops[:, 0:TT]))
            ve.tensor_tensor(tops3, tops3, small.rearrange("p (o t) -> p o t", o=1).to_broadcast([P, TOPK, TT]),
                             ALU.subtract).then_inc(s["rt_mask"], 1)
            done(ve.tensor_tensor(CAND, HOT[0], HOT[1], ALU.add))
            done(ve.tensor_tensor(CAND, CAND, HOT[2], ALU.add))
            ve.tensor_tensor(chosen, CAND, HOT[3], ALU.add).then_inc(s["rt_mask"], 1)
            ve.wait_ge(s["rt_act"], 2)
            done(ve.reduce_sum(small, tops.rearrange("p (k t) -> p t k", k=TOPK), axis=AX.X))
            done(ve.reciprocal(small, small))
            entry4 = entry[:, :].bitcast(f32).rearrange("p (t k w) -> p t k w", k=TOPK, w=4)
            done(ve.tensor_tensor(entry4[:, :, :, 1], tops.rearrange("p (k t) -> p t k", k=TOPK),
                                  small.rearrange("p (t o) -> p t o", o=1).to_broadcast([P, TT, TOPK]), ALU.mult))
            done(ve.tensor_copy(entry4[:, :, :, 2], rms.rearrange("p (t o) -> p t o", o=1).to_broadcast([P, TT, TOPK])))
            done(ve.memset(entry4[:, :, :, 3], 0.0))
            done(ve.memset(gains[:, 0:SHARED_TILES], 1.0))
            for j in range(SHARED):
                done(ve.tensor_copy(gains[:, GT + j * TT:GT + (j + 1) * TT], rms))
            et = lambda a: a.rearrange("p (e t) -> p e t", t=TT)
            by_te = lambda a: a.rearrange("p (e t) -> p t e", t=TT)
            done(ve.memset(RESET, 1.0))
            done(ve.memset(et(RESET)[:, :, 0:1], 0.0))
            ve.wait_ge(s["rt_pe"], 1)
            done(ve.tensor_copy(et(CNT), ps_z[:, :].rearrange("p (t e) -> p e t", e=EXPERTS)))
            done(ve.tensor_tensor_scan(INCL, RESET, CNT, 0.0, ALU.mult, ALU.add))
            done(ve.tensor_tensor(CNT, INCL, CNT, ALU.subtract))
            counts = et(INCL)[:, :, TT - 1:TT].to_broadcast([P, EXPERTS, TT])
            done(ve.tensor_tensor(et(CAND), counts, ramp128.rearrange("p (o t) -> p o t", o=1).to_broadcast([P, EXPERTS, TT]),
                                  ALU.is_gt))
            done(ve.reduce_sum(small, et(CAND), axis=AX.X))
            done(ve.tensor_scalar(small, small, 1.0, None, ALU.max))
            done(ve.memset(rampf, 1.0))
            done(ve.tensor_tensor_scan(ends, rampf, small, 0.0, ALU.mult, ALU.add))
            done(ve.tensor_tensor(small, ends, small, ALU.subtract))
            done(ve.tensor_scalar(small, small, float(P), None, ALU.mult))
            done(ve.memset(bounds[:, 0:1], 0))
            done(ve.tensor_copy(bounds[:, 1:EXPERTS + 1], ends))
            done(ve.tensor_tensor(te(LG), te(ps_x1[:, :]), by_te(CNT), ALU.add))
            done(ve.tensor_tensor(te(LG), te(LG), per_e(small), ALU.add))
            for k in range(TOPK):
                done(ve.tensor_tensor(CAND, HOT[k], LG, ALU.mult))
                done(ve.reduce_sum(small, te(CAND), axis=AX.X))
                done(ve.tensor_copy(where[:, :].rearrange("p (t k) -> p t k", k=TOPK)[:, :, k], small))
            ve.memset(small, 0.0).then_inc(s["entry_ready"], 1)

            def split_x(g):
                ve.wait_ge(s["x_hi"], g + 1)
                ve.tensor_tensor(xlo, ps_xt[:, :], xhi.bitcast(f32), ALU.subtract).then_inc(s["x_lo"], 1)

            def weights(j, g):
                for q in range(GROUPS):
                    ve.wait_ge(s["w_hi"], j * GROUPS + q + 1)
                    ve.tensor_tensor(wlo[:, q * GC:(q + 1) * GC], stage[:, q * GC:(q + 1) * GC],
                                     whi[:, q * GC:(q + 1) * GC].bitcast(f32), ALU.subtract).then_inc(s["w_lo"], 1)

            def tile(g, j):
                for a in range(2):
                    ve.wait_ge(s["silu_done"], g * 2 + a + 1)
                    part = act[:, a * 256:a * 256 + 256]
                    ve.scalar_tensor_tensor(part, ps_h[:, a * 512 + 256:a * 512 + 512], gains[:, ds(g + GT, 1)], part,
                                            ALU.mult, ALU.mult).then_inc(s["act_done"], 1)
                for a in range(2):
                    ve.wait_ge(s["a_hi"], g * 2 + a + 1)
                    ve.tensor_tensor(alo[:, a * 256:a * 256 + 256], ps_at[a],
                                     ahi[:, a * 256:a * 256 + 256].bitcast(f32), ALU.subtract).then_inc(s["a_lo"], 1)
                split_x(g + 1)
                ve.wait_ge(s["w2_read"], g * 2 + 3)
                ve.wait_ge(s["y_out"], (g + 1) * 16)
                ve.tensor_scalar(y[:, 512:1024], ps_y[:, 512:1024], gains[:, ds(g, 1)], None, ALU.mult).then_inc(s["y_lo"], 1)

            split_x(0)
            shared_loop(ve, weights, tile)
            ve.wait_ge(s["slots_in"], 16)
            slots3 = slots.bitcast(f32).rearrange("p (t w) -> p t w", w=4)
            ve.tensor_copy(gains[:, SHARED_TILES:GT], slots3[:, :, 1]).then_inc(s["gains_set"], 1)
            ve.tensor_copy(gains[:, GT + SHARED_TILES:2 * GT], slots3[:, :, 2]).then_inc(s["gains_set"], 1)
            ve.wait_ge(s["gains_set"], 2)
            routed_loop(ve, weights, tile)

        @block.tensor
        def _(pe):
            pe.wait_ge(s["masks"], 7)
            pe.wait_ge(s["consts_in"], 64)

            def linear(v, par, gated, o):
                pe.wait_ge(s["w0_lo"], v + 2)
                pe.wait_ge(s["w0_hi"], v + 1)
                pe.wait_ge(s["gated_lo"], gated)
                pe.wait_ge(s["gated_hi"], gated)
                pe.wait_ge(s["x1_pre"], v + 1)
                for c in range(CB):
                    for wpart, cpart in ((w0hi, C0HI), (w0hi, C0LO), (w0lo, C0HI)):
                        first = wpart is w0hi and cpart == C0HI and c == 0
                        final = wpart is w0lo and c == CB - 1
                        for h in range(2):
                            last = pe.matmul(ps_x1[:, h * 512:h * 512 + 512], wpart[:, c * P:(c + 1) * P],
                                             halves[:, ds(par * PAR + (cpart + c * SEQ + h * 512), 512)],
                                             start=first, stop=final)
                last.then_inc(s["ffn_done"], 1)
                pe.wait_ge(s["res"], v + 1)
                pe.wait_ge(s["r_copy"], v + 1)
                for t in range(ST):
                    last = pe.transpose(ps_r[:, t * P:(t + 1) * P], XL[:, t * P:(t + 1) * P], ident[:, :])
                last.then_inc(s["r_tr"], 1)
                pe.wait_ge(s["z"], v + 1)
                pe.wait_ge(s["z_copy"], v + 1)
                for t in range(ST):
                    last = pe.transpose(ps_z[:, t * P:(t + 1) * P], C1[:, t * P:(t + 1) * P], ident[:, :])
                last.then_inc(s["z_tr"], 1)
                pe.wait_ge(s["sq"], v + 1)
                pe.wait_ge(s["l_acc"], v + 1)
                for t in range(ST):
                    pe.matmul(ps_l[:, t * 33:t * 33 + 32], C1[:, t * P:(t + 1) * P], rw[:, ds(o * EXPERTS, EXPERTS)],
                              start=True, stop=True)
                    last = pe.matmul(ps_l[:, t * 33 + 32:t * 33 + 33], RL[:, t * P:(t + 1) * P], ones[:, :],
                                     start=True, stop=True)
                last.then_inc(s["l_mm"], 1)

            with pe.Fori(1, BATCH) as b:
                with pe.Fori(0, CB) as c:
                    linear(b * CB + c - CB, (b + 1) % 2, b * CB, c)
            with pe.Fori(0, CB) as c:
                linear(c + (BATCH - 1) * CB, (BATCH - 1) % 2, BLOCKS, c)

            pe.wait_ge(s["rt_mask"], 3)
            pe.wait_ge(s["z_copy"], BLOCKS + 1)
            for h in range(2):
                pe.matmul(ps_x1[:, h * 512:h * 512 + 512], before[:, :], chosen[:, h * 512:h * 512 + 512], start=True, stop=True)
            for h in range(2):
                last = pe.matmul(ps_z[:, h * 512:h * 512 + 512], allb[:, :], chosen[:, h * 512:h * 512 + 512], start=True, stop=True)
            last.then_inc(s["rt_pe"], 1)

            def transpose_x(g):
                pe.wait_ge(s["rows_in"], (g + 1) * 16)
                pe.wait_ge(s["x_lo"], g + 1)
                for c in range(CB):
                    last = pe.transpose(ps_xt[:, c * P:(c + 1) * P], hx[:, c * P:(c + 1) * P], ident[:, :])
                last.then_inc(s["x_tr"], 1)

            def transpose_act(g, a):
                pe.wait_ge(s["act_done"], g * 2 + a + 2)
                for i in range(2):
                    at = a * 256 + i * P
                    last = pe.transpose(ps_at[a][:, i * P:(i + 1) * P], act[:, at:at + P], ident[:, :])
                last.then_inc(s["a_tr"], 1)

            def weights(j, g):
                pass

            def tile(g, j):
                pe.wait_ge(s["x_lo"], g + 2)
                pe.wait_ge(s["act_done"], g * 2 + 1)
                for q in range(4):
                    a, kh = q // 2, q % 2
                    pe.wait_ge(s["w_lo"], j * GROUPS + q + 2)
                    for k in range(4):
                        xk = kh * 4 + k
                        rhs = slice(q * GC + k * 512, q * GC + k * 512 + 512)
                        for xp, wp in ((xhi, whi), (xhi, wlo), (xlo, whi)):
                            last = pe.matmul(ps_h[:, a * 512:a * 512 + 512], xp[:, xk * P:(xk + 1) * P], wp[:, rhs],
                                             start=(xk == 0 and xp is xhi and wp is whi), stop=(xk == 7 and xp is xlo))
                    last.then_inc(s["w1_read"], 1)
                transpose_act(g, 0)
                transpose_x(g + 1)
                transpose_act(g, 1)
                pe.wait_ge(s["y_lo"], g + 1)
                pe.wait_ge(s["y_hi"], g + 1)
                for q in range(2):
                    pe.wait_ge(s["w_lo"], j * GROUPS + q + 5 + 1)
                    pe.wait_ge(s["a_lo"], g * 2 + q + 1)
                    for k in range(2):
                        for ap_, wp in ((ahi, whi), (ahi, wlo), (alo, whi)):
                            for h in range(2):
                                rhs = (4 + q) * GC + k * 1024 + h * 512
                                last = pe.matmul(ps_y[:, h * 512:h * 512 + 512], ap_[:, (q * 2 + k) * P:(q * 2 + k + 1) * P],
                                                 wp[:, rhs:rhs + 512], start=(q == 0 and k == 0 and ap_ is ahi and wp is whi),
                                                 stop=(q == 1 and k == 1 and ap_ is alo))
                    last.then_inc(s["w2_read"], 1)

            transpose_x(0)
            shared_loop(pe, weights, tile)
            pe.wait_ge(s["entry_ready"], 1)
            routed_loop(pe, weights, tile)


def kernel(x, fside_BxSxS_0, cond_512, L0_cond_w, L0_cond_u, L0_ffn_weight, L0_ffn_scale_weight, L0_ffn_bias,
           L1_cond_w, L1_cond_u, L1_ffn_norm_w, L1_ffn_router_w, L1_ffn_w1, L1_ffn_w2, L1_ffn_sg, L1_ffn_su, L1_ffn_sd):
    import numpy as np
    import concourse.bacc as bacc
    from concourse.bass_utils import run_bass_kernel_spmd

    a = lambda v: np.asarray(v)
    by_partition = lambda v: a(v).reshape(CB, P).T
    blocks = lambda v: np.ascontiguousarray(a(v).transpose(0, 2, 1)).reshape(BLOCKS * P, SEQ)
    up = a(L1_ffn_w1)
    halves = lambda v: [v[:, i * INNER:(i + 1) * INNER] for i in range(SHARED)]
    shared_w1 = [np.concatenate(p, 1) for p in zip(halves(a(L1_ffn_sg)), halves(a(L1_ffn_su)))]
    w1 = np.concatenate([np.stack(shared_w1), up])
    w1 = w1.reshape(-1, 2, 4, P, 2, 2, 256).transpose(0, 5, 1, 3, 2, 4, 6).reshape(-1, 4, P, GC)
    w2 = np.concatenate([a(L1_ffn_sd).reshape(SHARED, INNER, CH), a(L1_ffn_w2)])
    w2 = w2.reshape(-1, 2, 2, P, CH).transpose(0, 1, 3, 2, 4).reshape(-1, 2, P, GC)
    expert_w = np.concatenate([w1, w2], 1).reshape(-1, GC)
    arrays = {
        "x_t": blocks(x),
        "side_t": blocks(fside_BxSxS_0),
        "cond": a(cond_512).reshape(1, -1),
        "w_u": np.stack([np.concatenate([by_partition(L0_cond_w), by_partition(L1_cond_w)], 1),
                         np.concatenate([by_partition(L0_cond_u), by_partition(L1_cond_u)], 1)]),
        "lin_w": a(L0_ffn_weight).reshape(CB, P, CB, P).transpose(0, 3, 2, 1).reshape(CB * P, CH),
        "lin_sb": np.concatenate([by_partition(L0_ffn_scale_weight), by_partition(L0_ffn_bias)], 1),
        "norm_w": by_partition(L1_ffn_norm_w),
        "router_t": a(L1_ffn_router_w).reshape(EXPERTS, CB, P).transpose(2, 1, 0).reshape(P, CB * EXPERTS),
        "expert_w": expert_w,
    }
    arrays = {k: np.ascontiguousarray(v) for k, v in arrays.items()}
    nc = bacc.Bacc("TRN2", target_bir_lowering=False, num_devices=1)
    ins = [nc.dram_tensor(k, v.shape, mybir.dt.from_np(v.dtype), kind="ExternalInput").ap() for k, v in arrays.items()]
    out = nc.dram_tensor("out", (TOK + P, CH), mybir.dt.float32, kind="ExternalOutput").ap()
    adaln_moe(nc, *ins, out)
    r = run_bass_kernel_spmd(nc, [arrays], core_ids=[0])
    return r.results[0]["out"][:TOK].reshape(BATCH, SEQ, CH)
```

```python
import concourse.bass as bass
from concourse import mybir
from contextlib import ExitStack
import numpy as np

BATCH, SEQ, CH, COND = 4, 1024, 1024, 256
EXPERTS, TOPK, INNER = 32, 4, 512
SHARED = 2
P = 128
CB = CH // P
TOK = BATCH * SEQ
TT = TOK // P
ST = SEQ // P
ROUTED_TILES = TOK * TOPK // P + 2 * (EXPERTS - TOPK - 1) + TOPK
SLOT_TILES = ROUTED_TILES + 2
SHARED_TILES = SHARED * TT
FILLS = 2
GROUPS = 6
GC = CB * 2 * INNER // 4
BLOCKS = BATCH * CB


def adaln_moe(nc, x_t, side_t, cond, w_u, lin_w, lin_sb, norm_w, router_t, expert_w, out):
    f32, f32r, bf16 = mybir.dt.float32, mybir.dt.float32r, mybir.dt.bfloat16
    i32, u32 = mybir.dt.int32, mybir.dt.uint32
    ALU, ACT, AX = mybir.AluOpType, mybir.ActivationFunctionType, mybir.AxisListType
    ds = bass.ds

    ratio_dram = nc.dram_tensor("ratio_dram", (BLOCKS * P, SEQ), f32).ap()
    rows_dram = nc.dram_tensor("rows_dram", (TOK + P, CH), f32).ap()
    slots_dram = nc.dram_tensor("slots_dram", (SLOT_TILES * P, 4), i32).ap()

    ctx = ExitStack()
    with ctx:
        def sb(name, cols, dt=f32):
            return ctx.enter_context(nc.sbuf_tensor(name, [P, cols], dt))

        def sem(name):
            return ctx.enter_context(nc.semaphore(name))

        halves = sb("halves", 34 * 1024, f32r)
        PAR = CB * SEQ
        C0HI, C0LO, W0HI, W0LO = 0, 2 * PAR, 4 * PAR, 4 * PAR + 1024
        EW = GROUPS * GC
        whi, wlo = halves[:, 0:EW], halves[:, EW:2 * EW]
        xhi, xlo = halves[:, 2 * EW:2 * EW + 1024], halves[:, 2 * EW + 1024:2 * EW + 2048]
        ahi, alo = halves[:, 2 * EW + 2048:2 * EW + 2560], halves[:, 2 * EW + 2560:2 * EW + 3072]
        w0hi, w0lo = halves[:, W0HI:W0HI + 1024], halves[:, W0LO:W0LO + 1024]

        WORK = EW + 2560 + 4 * SLOT_TILES
        work = sb("work", WORK)
        (K, X, EK, EKV, W, F, G, H, N, WST, XL, C1, RL, RS, ZS) = (
            work[:, i * 1024:(i + 1) * 1024] for i in range(15))
        stage = work[:, 0:EW]
        hx = work[:, EW:EW + 1024]
        y = work[:, EW + 1024:EW + 2048]
        act = work[:, EW + 2048:EW + 2560]
        slots = work[:, EW + 2560:EW + 2560 + 4 * SLOT_TILES].bitcast(i32)

        LG, CAND, RESET, CNT, INCL = X, EK, XL, C1, H
        HOT = [EKV, W, F, G]
        chosen = N[:, 0:512].bitcast(bf16)
        rms, small, rampf, rev, ramp128, ends = (WST[:, i * 32:(i + 1) * 32] for i in range(6))
        tops = WST[:, 256:256 + TOPK * TT]
        EXP30 = float(np.exp(np.float32(30.0)))

        acc = sb("acc", TT * 33)
        GT = SHARED_TILES + SLOT_TILES
        gains = acc[:, 0:2 * GT]
        decay = sb("decay", 2 * BLOCKS)
        uu = sb("uu", 2 * CB)
        ww = sb("ww", 2 * CB)
        lsb = sb("lsb", 2 * CB)
        nrm = sb("nrm", CB)
        rw = sb("rw", CB * EXPERTS)
        ident = sb("ident", P)
        ones = sb("ones", 1)
        before = sb("before", P, bf16)
        allb = sb("allb", P, bf16)
        tf = sb("tf", BATCH)
        half_tf = sb("half_tf", BATCH)
        neg_gain = sb("neg_gain", BATCH)
        entry = sb("entry", TT * TOPK * 4, i32)
        where = sb("where", TT * TOPK, i32)
        bounds = sb("bounds", EXPERTS + 1, i32)
        row_idx = sb("row_idx", 1, i32)
        add_idx = sb("add_idx", 1, i32)
        ramp = where[:, 0:EXPERTS]
        put_idx = sb("put_idx", TOPK, i32)
        put_val = sb("put_val", TOPK * 4, i32)

        ps = [ctx.enter_context(nc.psum_tensor(f"ps{i}", [P, 1024], f32)) for i in range(4)]
        ps_x1, ps_z, ps_r, ps_l = ps
        ps_h, ps_xt, ps_y = ps[0], ps[1], ps[2]
        ps_at = [ps[3][:, 0:256], ps[3][:, 512:768]]

        s = {}
        for name in (
            "k_in x_in ramp w0_in xl_in rl_in consts_in cond_in kc ek ekv euk w_diff h_fwd h_bwd h_sum h_all den "
            "g_ln g_inv nf nb n_sum wv_done num newton1 newton2 sig_x gated gated_hi gated_lo ratio ratio_out "
            "w0_hi w0_lo ffn_done x1_pre sig_x1 c1 res sq z r_tr z_tr l_mm r_copy z_copy r_out z_out l_acc "
            "prep prep_act masks rt rt_act rt_mask rt_pe fill_set add_idx_set gated_raw apart entry_ready put_set put_out "
            "slots_in gains_set w_hi w_lo w1_read w2_read rows_in row_idx_set x_tr x_hi x_lo h_mm "
            "silu_done act_done a_tr a_hi a_lo y_mm y_hi y_lo y_out zero_set zero_out"
        ).split():
            s[name] = sem(name)

        ONE_AHEAD = (
            "wv_done gated w0_lo r_tr l_mm ratio_out w_lo ffn_done num z_tr r_out z_out a_tr "
            "w1_read w2_read x1_pre r_copy z_copy l_acc act_done x_lo y_lo y_hi"
        ).split()
        w_in = [sem(f"w_in{q}") for q in range(GROUPS)]
        block = ctx.enter_context(nc.Block())

        def apart(eng):
            eng.sem_inc(s["apart"], 1)

        def expert_loop(eng, tile, last_tile, between=None):
            with eng.Fori(0, SHARED) as j:
                with eng.Fori(j * TT, j * TT + (TT - 1)) as g:
                    tile(g, j)
                last_tile(j * TT + (TT - 1), j)
            if between:
                between()
            eng.wait_ge(s["gains_set"], 2)

            def group(e, j, last_tile):
                first = eng.value_load(bounds[0:1, ds(e, 1)], min_val=0, max_val=ROUTED_TILES)
                end = eng.value_load(bounds[0:1, ds(e + 1, 1)], min_val=2, max_val=ROUTED_TILES)
                with eng.Fori(first + SHARED_TILES, end + (SHARED_TILES - 1)) as g:
                    tile(g, j)
                last_tile(end + (SHARED_TILES - 1), j)

            with eng.Fori(0, EXPERTS - 1) as e:
                group(e, e + SHARED, last_tile)
            group(EXPERTS - 1, SHARED + EXPERTS - 1, tile)

        @block.sync
        def _(sp):
            for name in ONE_AHEAD:
                sp.sem_inc(s[name], 1)
            sp.dma_start(ww[:, :], w_u[0]).then_inc(s["cond_in"], 16)
            sp.dma_start(work[:, 0:BATCH * COND], cond.to_broadcast([P, BATCH * COND])).then_inc(s["cond_in"], 16)
            for dst, src in ((uu, w_u[1]), (lsb, lin_sb), (nrm, norm_w), (rw, router_t)):
                sp.dma_start(dst[:, :], src).then_inc(s["consts_in"], 16)

            def store_ratio(u):
                sp.wait_ge(s["ratio"], u + 1)
                sp.dma_start(ratio_dram[ds(u * P, P), :], N).then_inc(s["ratio_out"], 16)

            def store_rows(v, b, o):
                rows = out[ds(b * SEQ, SEQ), ds(o * P, P)].rearrange("(t p) c -> p t c", p=P)
                sp.wait_ge(s["r_copy"], v + 2)
                sp.dma_start(rows, RS.rearrange("p (t c) -> p t c", c=P)).then_inc(s["r_out"], 16)
                rows = rows_dram[ds(b * SEQ, SEQ), ds(o * P, P)].rearrange("(t p) c -> p t c", p=P)
                sp.wait_ge(s["z_copy"], v + 2)
                sp.dma_start(rows, ZS.rearrange("p (t c) -> p t c", c=P)).then_inc(s["z_out"], 16)

            with sp.Fori(0, CB) as u:
                store_ratio(u)
            with sp.Fori(1, BATCH) as b:
                with sp.Fori(0, CB) as c:
                    store_rows((b - 1) * CB + c, b - 1, c)
                    store_ratio(b * CB + c)
            with sp.Fori(0, CB) as c:
                store_rows((BATCH - 1) * CB + c, BATCH - 1, c)

            sp.wait_ge(s["zero_set"], 1)
            sp.dma_start(rows_dram[TOK:TOK + P, :], K).then_inc(s["zero_out"], 16)
            sp.wait_ge(s["zero_out"], 16)
            sp.wait_ge(s["y_out"], 16)
            sp.wait_ge(s["entry_ready"], 1)

            def load_weights(j):
                for q in range(GROUPS):
                    sp.wait_ge(s["w_lo"], j * GROUPS + q - (GROUPS - 2))
                    sp.dma_start(stage[:, q * GC:(q + 1) * GC],
                                 expert_w[ds((j * GROUPS + q) * P, P), :]).then_inc(w_in[q], 16)

            for q in range(GROUPS):
                sp.dma_start(stage[:, q * GC:(q + 1) * GC], expert_w[q * P:(q + 1) * P, :]).then_inc(w_in[q], 16)
            for j in range(1, SHARED):
                load_weights(j)
            sp.wait_ge(s["put_out"], 16 * (TT * TOPK + FILLS))
            sp.dma_start(slots.rearrange("p (t w) -> p t w", w=4),
                         slots_dram.rearrange("(t p) w -> p t w", p=P)).then_inc(s["slots_in"], 16)
            with sp.Fori(SHARED, SHARED + EXPERTS) as j:
                load_weights(j)

        @block.gpsimd
        def _(pool):
            pool.memset(ident[:, :], 0.0).then_inc(s["masks"], 1)
            pool.memset(allb[:, :], 1.0).then_inc(s["masks"], 1)
            pool.memset(before[:, :], 1.0).then_inc(s["masks"], 1)
            pool.memset(ones[:, :], 1.0).then_inc(s["masks"], 1)
            pool.memset(acc[:, :], 0.0).then_inc(s["masks"], 1)
            pool.wait_ge(s["masks"], 5)
            pool.affine_select(out=ident[:, :], in_=ident[:, :], compare_op=ALU.not_equal, fill=1.0,
                               base=0, pattern=[[-1, P]], channel_multiplier=1).then_inc(s["masks"], 1)
            pool.affine_select(out=before[:, :], in_=before[:, :], compare_op=ALU.is_gt, fill=0.0,
                               base=0, pattern=[[1, P]], channel_multiplier=-1).then_inc(s["masks"], 1)


            pool.iota(ramp, pattern=[[1, EXPERTS]], base=0, channel_multiplier=0).then_inc(s["ramp"], 1)
            pool.iota(entry[:, :].rearrange("p (t k w) -> p t k w", k=TOPK, w=4)[:, :, :, 0],
                      pattern=[[P, TT], [0, TOPK]], base=0, channel_multiplier=1).then_inc(s["ramp"], 1)
            def load_side(u):
                pool.wait_ge(s["wv_done"], 2 * u + 1)
                apart(pool)
                pool.dma_start(K, side_t[ds(u * P, P), :]).then_inc(s["k_in"], 16)

            def load_x(u):
                pool.wait_ge(s["gated"], u + 1)
                apart(pool)
                pool.dma_start(X, x_t[ds(u * P, P), :]).then_inc(s["x_in"], 16)

            def load_w0(v, o):
                pool.wait_ge(s["w0_lo"], v + 1)
                apart(pool)
                pool.dma_start(WST, lin_w[ds(o * P, P), :]).then_inc(s["w0_in"], 16)

            def load_xl(v):
                pool.wait_ge(s["r_tr"], v + 1)
                apart(pool)
                pool.dma_start(XL, x_t[ds(v * P, P), :]).then_inc(s["xl_in"], 16)

            def load_ratio(v):
                pool.wait_ge(s["l_mm"], v + 1)
                pool.wait_ge(s["ratio_out"], (v + 1) * 16 + 1)
                apart(pool)
                pool.dma_start(RL, ratio_dram[ds(v * P, P), :]).then_inc(s["rl_in"], 16)

            pool.wait_ge(s["prep"], 1)
            with pool.Fori(0, CB) as u:
                load_x(u)
                load_side(u)
            with pool.Fori(1, BATCH) as b:
                with pool.Fori(0, CB) as c:
                    load_w0(b * CB + c - CB, c)
                    load_x(b * CB + c)
                    load_xl(b * CB + c - CB)
                    load_side(b * CB + c)
                    load_ratio(b * CB + c - CB)
            with pool.Fori(0, CB) as c:
                load_w0(c + (BATCH - 1) * CB, c)
                load_xl(c + (BATCH - 1) * CB)
                load_ratio(c + (BATCH - 1) * CB)

            pool.wait_ge(s["z_out"], 16 * BLOCKS + 1)
            pool.wait_ge(s["r_out"], 16 * BLOCKS + 1)
            pool.memset(slots, 0).then_inc(s["fill_set"], 1)
            pool.wait_ge(s["fill_set"], 1)
            pool.iota(slots.rearrange("p (t w) -> p t w", w=4)[:, :, 0], pattern=[[0, SLOT_TILES]],
                      base=TOK, channel_multiplier=1).then_inc(s["fill_set"], 1)
            pool.wait_ge(s["fill_set"], 2)
            for t in range(0, SLOT_TILES, SLOT_TILES // FILLS):
                n = SLOT_TILES // FILLS
                pool.dma_start(slots_dram[t * P:(t + n) * P, :].rearrange("(t p) w -> p t w", p=P),
                               slots[:, 4 * t:4 * (t + n)].rearrange("p (t w) -> p t w", w=4)).then_inc(s["put_out"], 16)
            pool.wait_ge(s["zero_set"], 1)
            pool.dma_start(out[TOK:TOK + P, :], K).then_inc(s["y_out"], 16)

            def load_rows(t):
                apart(pool)
                pool.dma_start(hx, rows_dram[ds(t * P, P), :]).then_inc(s["rows_in"], 16)

            def gather_rows(g):
                pool.tensor_copy(row_idx[:, :], slots[:, ds((g - SHARED_TILES) * 4, 1)]).then_inc(s["row_idx_set"], 1)
                pool.wait_ge(s["row_idx_set"], g - (SHARED_TILES - 1))
                apart(pool)
                pool.indirect_dma_start(hx, None, rows_dram[:, :],
                                        bass.IndirectOffsetOnAxis(row_idx[:, :].bitcast(u32), 0)).then_inc(s["rows_in"], 16)

            def await_y(g):
                pool.wait_ge(s["y_hi"], g + 2)
                pool.wait_ge(s["y_lo"], g + 2)
                pool.wait_ge(s["y_out"], 16 * (g + 1))

            def add_rows(g, t):
                await_y(g)
                apart(pool)
                pool.dma_start(out[ds(t * P, P), :], y, accum_op=ALU.add).then_inc(s["y_out"], 16)

            def put_entries(t):
                pool.wait_ge(s["put_out"], 16 * (TOPK * t + FILLS))
                pool.tensor_copy(put_idx[:, :], where[:, ds(t * TOPK, TOPK)]).then_inc(s["put_set"], 1)
                pool.tensor_copy(put_val[:, :], entry[:, ds(t * TOPK * 4, TOPK * 4)]).then_inc(s["put_set"], 1)
                pool.wait_ge(s["put_set"], 2 * t + 2)
                for k in range(TOPK):
                    apart(pool)
                    pool.indirect_dma_start(slots_dram[:, :], bass.IndirectOffsetOnAxis(put_idx[:, k:k + 1].bitcast(u32), 0),
                                            put_val[:, 4 * k:4 * k + 4], None).then_inc(s["put_out"], 16)

            pool.wait_ge(s["zero_out"], 16)
            pool.wait_ge(s["entry_ready"], 1)
            load_rows(0)
            pool.wait_ge(s["x_tr"], 1)
            load_rows(1)
            with pool.Fori(0, TT) as g:
                put_entries(g)
                pool.wait_ge(s["x_tr"], g + 2)
                load_rows((g + 2) % TT)
                add_rows(g, g)
            with pool.Fori(0, TT - 2) as t:
                pool.wait_ge(s["x_tr"], t + (TT + 2))
                load_rows(t + 2)
                add_rows(t + TT, t)
            pool.wait_ge(s["slots_in"], 16)
            for g in range(SHARED_TILES - 2, SHARED_TILES):
                pool.wait_ge(s["x_tr"], g + 2)
                gather_rows(g + 2)
                add_rows(g, g - TT)
            tiles = pool.value_load(bounds[0:1, EXPERTS:EXPERTS + 1], min_val=EXPERTS, max_val=ROUTED_TILES)
            with pool.Fori(SHARED_TILES, tiles + SHARED_TILES) as g:
                pool.wait_ge(s["x_tr"], g + 2)
                gather_rows(g + 2)
                await_y(g)
                pool.tensor_copy(add_idx[:, :], slots[:, ds((g - SHARED_TILES) * 4, 1)]).then_inc(s["add_idx_set"], 1)
                pool.wait_ge(s["add_idx_set"], g - (SHARED_TILES - 1))
                apart(pool)
                pool.indirect_dma_start(out[:, :], bass.IndirectOffsetOnAxis(add_idx[:, :].bitcast(u32), 0),
                                        y, None, compute_op=ALU.add).then_inc(s["y_out"], 16)
            pool.wait_ge(s["rows_in"], (tiles + (SHARED_TILES + 2)) * 16)
            pool.wait_ge(s["y_out"], (tiles + (SHARED_TILES + 1)) * 16)

        @block.scalar
        def _(sc):
            sc.wait_ge(s["prep"], 1)
            sc.activation(tf[:, :], tf[:, :], ACT.Sigmoid).then_inc(s["prep_act"], 1)
            sc.wait_ge(s["cond_in"], 32)
            sc.activation(ww[:, :], ww[:, :], ACT.Exp).then_inc(s["prep_act"], 1)
            sc.wait_ge(s["prep_act"], 2)
            sc.activation(ww[:, :], ww[:, :], ACT.Exp, scale=-1.0).then_inc(s["prep_act"], 1)

            def unit(u, c, par, freed, linear=None):
                if linear:
                    linear.split()
                sc.wait_ge(s["kc"], u + 1)
                sc.activation(EK, EK, ACT.Exp).then_inc(s["ek"], 1)

                def euk(l):
                    sc.wait_ge(s["num"], u * 2 + l + 1)
                    apart(sc)
                    sc.activation(W, K, ACT.Exp, bias=uu[:, ds(c + l * CB, 1)]).then_inc(s["euk"], 1)

                def inverse(l):
                    sc.wait_ge(s["den"], u * 2 + l + 1)
                    sc.activation(G, H, ACT.Ln).then_inc(s["g_ln"], 1)
                    sc.wait_ge(s["g_ln"], u * 2 + l + 1)
                    sc.activation(G, G, ACT.Exp, scale=-1.0).then_inc(s["g_inv"], 1)

                euk(0)
                inverse(0)
                sc.wait_ge(s["x_in"], (u + 1) * 16)
                sc.activation(X, X, ACT.Sigmoid).then_inc(s["sig_x"], 1)
                if linear:
                    linear.sigmoid()
                sc.preload_act_table_set("natural_log_exp_and_others")
                euk(1)
                sc.wait_ge(s["gated"], u + 2)
                if freed is not None:
                    sc.wait_ge(s["ffn_done"], freed + 1)
                apart(sc)
                sc.activation(halves[:, ds(c * SEQ + par * PAR + C0HI, SEQ)], N, ACT.Copy).then_inc(s["gated_hi"], 1)
                if linear:
                    linear.square()
                    linear.copies()
                inverse(1)

            class Linear:
                def __init__(self, v, o):
                    self.v, self.o = v, o

                def split(self):
                    sc.wait_ge(s["w0_in"], (self.v + 1) * 16)
                    sc.wait_ge(s["ffn_done"], self.v + 1)
                    sc.activation(w0hi, WST, ACT.Copy).then_inc(s["w0_hi"], 1)

                def sigmoid(self):
                    sc.wait_ge(s["x1_pre"], self.v + 2)
                    sc.wait_ge(s["z_tr"], self.v + 1)
                    sc.wait_ge(s["l_mm"], self.v + 1)
                    apart(sc)
                    sc.activation(C1, XL, ACT.Sigmoid, bias=lsb[:, ds(self.o + CB, 1)]).then_inc(s["sig_x1"], 1)

                def square(self):
                    sc.wait_ge(s["c1"], self.v + 1)
                    sc.activation(RL, C1, ACT.Square).then_inc(s["sq"], 1)

                def copies(self):
                    sc.wait_ge(s["r_tr"], self.v + 2)
                    sc.wait_ge(s["r_out"], self.v * 16 + 1)
                    sc.activation(RS, ps_r[:, :], ACT.Copy).then_inc(s["r_copy"], 1)
                    sc.wait_ge(s["z_tr"], self.v + 2)
                    sc.wait_ge(s["z_out"], self.v * 16 + 1)
                    sc.activation(ZS, ps_z[:, :], ACT.Copy).then_inc(s["z_copy"], 1)

            sc.wait_ge(s["consts_in"], 64)
            sc.preload_act_table_set("natural_log_exp_and_others")
            with sc.Fori(0, CB) as c:
                unit(c, c, 0, None)
            with sc.Fori(1, BATCH) as b:
                with sc.Fori(0, CB) as c:
                    unit(b * CB + c, c, b % 2, b * CB - CB, Linear(b * CB + c - CB, c))
            with sc.Fori(0, CB) as c:
                last = Linear(c + (BATCH - 1) * CB, c)
                last.split()
                last.sigmoid()
                last.square()
                last.copies()

            sc.wait_ge(s["rt_mask"], 1)
            sc.activation(rms, rms, ACT.Sqrt).then_inc(s["rt_act"], 1)
            sc.wait_ge(s["rt_mask"], 2)
            sc.activation(tops, tops, ACT.Exp).then_inc(s["rt_act"], 1)

            def split_x(g):
                sc.wait_ge(s["x_tr"], g + 1)
                sc.activation(xhi, ps_xt[:, :], ACT.Copy).then_inc(s["x_hi"], 1)

            def split_weights(j, q, g):
                sc.wait_ge(w_in[q], (j + 1) * 16)
                if g is not None:
                    sc.wait_ge(s["w1_read"] if q < 4 else s["w2_read"], g * 4 + (q - 2) if q < 4 else g * 2 + (q - 4))
                sc.activation(whi[:, q * GC:(q + 1) * GC], stage[:, q * GC:(q + 1) * GC],
                              ACT.Copy).then_inc(s["w_hi"], 1)

            def silu(g, a):
                sc.wait_ge(s["w1_read"], g * 4 + 2 * a + 3)
                sc.wait_ge(s["a_tr"], g * 2 + 1)
                apart(sc)
                sc.activation(act[:, a * 256:a * 256 + 256], ps_h[:, a * 512:a * 512 + 256], ACT.Silu,
                              scale=gains[:, ds(g + GT, 1)]).then_inc(s["silu_done"], 1)

            def split_act(g, a):
                sc.wait_ge(s["a_tr"], g * 2 + a + 2)
                sc.wait_ge(s["w2_read"], g * 2 + 1)
                sc.activation(ahi[:, a * 256:a * 256 + 256], ps_at[a], ACT.Copy).then_inc(s["a_hi"], 1)

            def weigh(g):
                sc.wait_ge(s["w2_read"], g * 2 + 3)
                sc.wait_ge(s["y_out"], (g + 1) * 16)
                apart(sc)
                sc.activation(y[:, 0:512], ps_y[:, 0:512], ACT.Copy, scale=gains[:, ds(g, 1)]).then_inc(s["y_hi"], 1)

            def tile(g, j):
                silu(g, 0)
                silu(g, 1)
                split_act(g, 0)
                split_act(g, 1)
                split_x(g + 1)
                weigh(g)

            def last_tile(g, j):
                silu(g, 0)
                split_weights(j + 1, 0, g + 1)
                split_weights(j + 1, 1, g + 1)
                silu(g, 1)
                split_act(g, 0)
                split_act(g, 1)
                split_x(g + 1)
                split_weights(j + 1, 2, g + 1)
                split_weights(j + 1, 3, g + 1)
                weigh(g)
                split_weights(j + 1, 4, g + 1)
                split_weights(j + 1, 5, g + 1)

            for q in range(GROUPS):
                split_weights(0, q, None)
            split_x(0)
            expert_loop(sc, tile, last_tile)

        @block.vector
        def _(ve):
            ve.wait_ge(s["cond_in"], 32)
            ve.reduce_sum(tf[:, :], work[:, 0:BATCH * COND].rearrange("p (b d) -> p b d", b=BATCH),
                          axis=AX.X).then_inc(s["prep"], 1)
            ve.wait_ge(s["prep_act"], 3)
            ve.tensor_scalar(half_tf[:, :], tf[:, :], 0.5, 0.5, ALU.mult, ALU.add).then_inc(s["prep"], 1)
            ve.tensor_scalar(neg_gain[:, :], tf[:, :], -0.2, -0.8, ALU.mult, ALU.add).then_inc(s["prep"], 1)
            ve.wait_ge(s["prep"], 3)
            for l in range(2):
                for b in range(BATCH):
                    ve.tensor_scalar(decay[:, l * BLOCKS + b * CB:l * BLOCKS + (b + 1) * CB], ww[:, l * CB:(l + 1) * CB],
                                     half_tf[:, b:b + 1], None, ALU.mult).then_inc(s["prep"], 1)
            ve.wait_ge(s["prep"], 3 + 2 * BATCH)
            ve.wait_ge(s["consts_in"], 64)

            def unit(u, b, c, par, linear=None):
                ve.wait_ge(s["k_in"], (u + 1) * 16)
                ve.tensor_scalar(EK, K, 30.0, None, ALU.min).then_inc(s["kc"], 1)
                if linear:
                    linear.split()
                ve.wait_ge(s["ek"], u + 1)
                ve.tensor_tensor(EKV, EK, K, ALU.mult).then_inc(s["ekv"], 1)
                for l in range(2):
                    n = u * 2 + l
                    d = decay[:, ds(u + l * BLOCKS, 1)].to_broadcast([P, SEQ])
                    ve.tensor_tensor_scan(H, d, EK, 0.0, ALU.mult, ALU.add).then_inc(s["h_fwd"], 1)
                    ve.tensor_tensor_scan(G[:, ::-1], d, EK[:, ::-1], 0.0, ALU.mult, ALU.add).then_inc(s["h_bwd"], 1)
                    ve.wait_ge(s["euk"], n + 1)
                    ve.scalar_tensor_tensor(W, W, EXP30, EK, ALU.min, ALU.subtract).then_inc(s["w_diff"], 1)
                    if linear and l == 1:
                        linear.gate()
                    if l == 0:
                        ve.wait_ge(s["ekv"], u + 1)
                    ve.tensor_tensor_scan(F, d, EKV, 0.0, ALU.mult, ALU.add).then_inc(s["nf"], 1)
                    ve.wait_ge(s["h_bwd"], n + 1)
                    ve.wait_ge(s["h_fwd"], n + 1)
                    ve.tensor_tensor(H, H, G, ALU.add).then_inc(s["h_sum"], 1)
                    if l == 0:
                        ve.wait_ge(s["ratio_out"], u * 16 + 1)
                    else:
                        if linear:
                            linear.residual()
                        ve.wait_ge(s["gated_hi"], u + 1)
                        ve.tensor_tensor(halves[:, ds(c * SEQ + par * PAR + C0LO, SEQ)], N,
                                         halves[:, ds(c * SEQ + par * PAR + C0HI, SEQ)].bitcast(f32),
                                         ALU.subtract).then_inc(s["gated_lo"], 1)
                        ve.wait_ge(s["gated_lo"], u + 1)
                    ve.tensor_tensor_scan(N[:, ::-1], d, EKV[:, ::-1], 0.0, ALU.mult, ALU.add).then_inc(s["nb"], 1)
                    ve.wait_ge(s["h_sum"], n + 1)
                    ve.wait_ge(s["w_diff"], n + 1)
                    ve.tensor_tensor(H, H, W, ALU.add).then_inc(s["h_all"], 1)
                    if linear and l == 1:
                        linear.scale()
                    ve.wait_ge(s["nf"], n + 1)
                    ve.wait_ge(s["nb"], n + 1)
                    ve.tensor_tensor(F, F, N, ALU.add).then_inc(s["n_sum"], 1)
                    ve.wait_ge(s["h_all"], n + 1)
                    ve.tensor_scalar(H, H, 1e-8, None, ALU.max).then_inc(s["den"], 1)
                    ve.tensor_tensor(W, W, K, ALU.mult).then_inc(s["wv_done"], 1)
                    ve.wait_ge(s["n_sum"], n + 1)
                    ve.wait_ge(s["wv_done"], n + 2)
                    ve.tensor_tensor(F, F, W, ALU.add).then_inc(s["num"], 1)
                    if linear and l == 0:
                        linear.add_x()
                    ve.wait_ge(s["g_inv"], n + 1)
                    ve.wait_ge(s["den"], n + 1)
                    ve.tensor_tensor(N, H, G, ALU.mult).then_inc(s["newton1"], 1)
                    ve.wait_ge(s["newton1"], n + 1)
                    ve.scalar_tensor_tensor(N, N, 2.0, G, ALU.subtract, ALU.mult).then_inc(s["newton2"], 1)
                    ve.wait_ge(s["newton2"], n + 1)
                    ve.wait_ge(s["num"], n + 2)
                    ve.scalar_tensor_tensor(N, F, neg_gain[:, ds(b, 1)] if not isinstance(b, int) else neg_gain[:, b:b + 1],
                                            N, ALU.mult, ALU.mult).then_inc(s["gated_raw"] if l == 0 else s["ratio"], 1)
                    if l == 0:
                        ve.wait_ge(s["gated_raw"], u + 1)
                        ve.wait_ge(s["sig_x"], u + 1)
                        ve.tensor_tensor(N, N, X, ALU.mult).then_inc(s["gated"], 1)
                if linear:
                    linear.logits()

            class Linear:

                def __init__(self, v, b, o):
                    self.v, self.b, self.o = v, b, o

                def split(self):
                    ve.wait_ge(s["w0_hi"], self.v + 1)
                    ve.tensor_tensor(w0lo, WST, w0hi.bitcast(f32), ALU.subtract).then_inc(s["w0_lo"], 1)

                def add_x(self):
                    ve.wait_ge(s["ffn_done"], self.v + 2)
                    ve.wait_ge(s["xl_in"], (self.v + 1) * 16)
                    ve.scalar_tensor_tensor(XL, ps_x1[:, :], lsb[:, ds(self.o, 1)], XL, ALU.mult, ALU.add)\
                        .then_inc(s["x1_pre"], 1)

                def gate(self):
                    ve.wait_ge(s["sig_x1"], self.v + 1)
                    ve.wait_ge(s["rl_in"], (self.v + 1) * 16)
                    ve.tensor_tensor(C1, C1, RL, ALU.mult).then_inc(s["c1"], 1)

                def residual(self):
                    ve.wait_ge(s["c1"], self.v + 1)
                    ve.scalar_tensor_tensor(XL, XL, lsb[:, ds(self.o + CB, 1)], C1, ALU.add, ALU.add).then_inc(s["res"], 1)

                def scale(self):
                    ve.wait_ge(s["sq"], self.v + 1)
                    ve.tensor_scalar(C1, C1, nrm[:, ds(self.o, 1)], None, ALU.mult).then_inc(s["z"], 1)

                def logits(self):
                    ve.wait_ge(s["l_mm"], self.v + 2)
                    ve.wait_ge(s["l_acc"], self.v + 1)
                    part = acc[:, ds(self.b * (ST * 33), ST * 33)]
                    ve.tensor_tensor(part, ps_l[:, 0:ST * 33], part, ALU.add).then_inc(s["l_acc"], 1)

            ve.wait_ge(s["masks"], 5)
            with ve.Fori(0, CB) as c:
                unit(c, 0, c, 0)
            with ve.Fori(1, BATCH) as b:
                with ve.Fori(0, CB) as c:
                    unit(b * CB + c, b, c, b % 2, Linear(b * CB + c - CB, b - 1, c))
            with ve.Fori(0, CB) as c:
                last = Linear(c + (BATCH - 1) * CB, BATCH - 1, c)
                last.split()
                last.add_x()
                last.gate()
                last.residual()
                last.scale()
                last.logits()

            ve.wait_ge(s["ratio_out"], 16 * BLOCKS + 1)
            ve.memset(K, 0.0).then_inc(s["zero_set"], 1)
            ve.wait_ge(s["ramp"], 2)
            ve.wait_ge(s["r_tr"], BLOCKS + 1)
            ve.wait_ge(s["z_tr"], BLOCKS + 1)
            steps = [0]

            def done(instruction):
                steps[0] += 1
                instruction.then_inc(s["rt"], 1)
                ve.wait_ge(s["rt"], steps[0])

            te = lambda a: a.rearrange("p (t e) -> p t e", e=EXPERTS)
            per_t = lambda a: a.rearrange("p (t o) -> p t o", o=1).to_broadcast([P, TT, EXPERTS])
            per_e = lambda a: a.rearrange("p (o e) -> p o e", o=1).to_broadcast([P, TT, EXPERTS])
            acc3 = acc[:, :].rearrange("p (t e) -> p t e", e=EXPERTS + 1)
            ve.wait_ge(s["l_acc"], BLOCKS + 1)
            done(ve.tensor_copy(rampf, ramp))
            done(ve.tensor_scalar(rev, rampf, -1.0, float(EXPERTS), ALU.mult, ALU.add))
            done(ve.tensor_scalar(ramp128, rampf, float(P), None, ALU.mult))
            ve.tensor_scalar(rms, acc3[:, :, EXPERTS], 1.0 / CH, 1e-6, ALU.mult, ALU.add).then_inc(s["rt_mask"], 1)
            ve.wait_ge(s["rt_act"], 1)
            done(ve.reciprocal(rms, rms))
            done(ve.tensor_tensor(te(LG), acc3[:, :, 0:EXPERTS], per_t(rms), ALU.mult))
            for k in range(TOPK):
                top = tops[:, k * TT:(k + 1) * TT]
                done(ve.reduce_max(top, te(LG), axis=AX.X))
                done(ve.tensor_tensor(te(CAND), te(LG), per_t(top), ALU.is_equal))
                done(ve.tensor_tensor(te(CAND), te(CAND), per_e(rev), ALU.mult))
                done(ve.reduce_max(small, te(CAND), axis=AX.X))
                done(ve.tensor_tensor(te(HOT[k]), te(CAND), per_t(small), ALU.is_equal))
                done(ve.scalar_tensor_tensor(LG, HOT[k], -1e30, LG, ALU.mult, ALU.add))
            tops3 = tops.rearrange("p (k t) -> p k t", k=TOPK)
            first = tops[:, 0:TT].rearrange("p (o t) -> p o t", o=1).to_broadcast([P, TOPK, TT])
            done(ve.tensor_copy(small, tops[:, 0:TT]))
            ve.tensor_tensor(tops3, tops3, small.rearrange("p (o t) -> p o t", o=1).to_broadcast([P, TOPK, TT]),
                             ALU.subtract).then_inc(s["rt_mask"], 1)
            done(ve.tensor_tensor(CAND, HOT[0], HOT[1], ALU.add))
            done(ve.tensor_tensor(CAND, CAND, HOT[2], ALU.add))
            ve.tensor_tensor(chosen, CAND, HOT[3], ALU.add).then_inc(s["rt_mask"], 1)
            ve.wait_ge(s["rt_act"], 2)
            done(ve.reduce_sum(small, tops.rearrange("p (k t) -> p t k", k=TOPK), axis=AX.X))
            done(ve.reciprocal(small, small))
            entry4 = entry[:, :].bitcast(f32).rearrange("p (t k w) -> p t k w", k=TOPK, w=4)
            done(ve.tensor_tensor(entry4[:, :, :, 1], tops.rearrange("p (k t) -> p t k", k=TOPK),
                                  small.rearrange("p (t o) -> p t o", o=1).to_broadcast([P, TT, TOPK]), ALU.mult))
            done(ve.tensor_copy(entry4[:, :, :, 2], rms.rearrange("p (t o) -> p t o", o=1).to_broadcast([P, TT, TOPK])))
            done(ve.memset(entry4[:, :, :, 3], 0.0))
            done(ve.memset(gains[:, 0:SHARED_TILES], 1.0))
            for j in range(SHARED):
                done(ve.tensor_copy(gains[:, GT + j * TT:GT + (j + 1) * TT], rms))
            et = lambda a: a.rearrange("p (e t) -> p e t", t=TT)
            by_te = lambda a: a.rearrange("p (e t) -> p t e", t=TT)
            done(ve.memset(RESET, 1.0))
            done(ve.memset(et(RESET)[:, :, 0:1], 0.0))
            ve.wait_ge(s["rt_pe"], 1)
            done(ve.tensor_copy(et(CNT), ps_z[:, :].rearrange("p (t e) -> p e t", e=EXPERTS)))
            done(ve.tensor_tensor_scan(INCL, RESET, CNT, 0.0, ALU.mult, ALU.add))
            done(ve.tensor_tensor(CNT, INCL, CNT, ALU.subtract))
            counts = et(INCL)[:, :, TT - 1:TT].to_broadcast([P, EXPERTS, TT])
            done(ve.tensor_tensor(et(CAND), counts, ramp128.rearrange("p (o t) -> p o t", o=1).to_broadcast([P, EXPERTS, TT]),
                                  ALU.is_gt))
            done(ve.reduce_sum(small, et(CAND), axis=AX.X))
            done(ve.tensor_scalar(small, small, 2.0, None, ALU.max))
            done(ve.memset(rampf, 1.0))
            done(ve.tensor_tensor_scan(ends, rampf, small, 0.0, ALU.mult, ALU.add))
            done(ve.tensor_tensor(small, ends, small, ALU.subtract))
            done(ve.tensor_scalar(small, small, float(P), None, ALU.mult))
            done(ve.memset(bounds[:, 0:1], 0))
            done(ve.tensor_copy(bounds[:, 1:EXPERTS + 1], ends))
            done(ve.tensor_tensor(te(LG), te(ps_x1[:, :]), by_te(CNT), ALU.add))
            done(ve.tensor_tensor(te(LG), te(LG), per_e(small), ALU.add))
            for k in range(TOPK):
                done(ve.tensor_tensor(CAND, HOT[k], LG, ALU.mult))
                done(ve.reduce_sum(small, te(CAND), axis=AX.X))
                done(ve.tensor_copy(where[:, :].rearrange("p (t k) -> p t k", k=TOPK)[:, :, k], small))
            ve.memset(small, 0.0).then_inc(s["entry_ready"], 1)

            def split_x(g):
                ve.wait_ge(s["x_hi"], g + 1)
                ve.tensor_tensor(xlo, ps_xt[:, :], xhi.bitcast(f32), ALU.subtract).then_inc(s["x_lo"], 1)

            def split_weights(j, q):
                ve.wait_ge(s["w_hi"], j * GROUPS + q + 1)
                ve.tensor_tensor(wlo[:, q * GC:(q + 1) * GC], stage[:, q * GC:(q + 1) * GC],
                                 whi[:, q * GC:(q + 1) * GC].bitcast(f32), ALU.subtract).then_inc(s["w_lo"], 1)

            def gate_up(g, a):
                ve.wait_ge(s["silu_done"], g * 2 + a + 1)
                part = act[:, a * 256:a * 256 + 256]
                ve.scalar_tensor_tensor(part, ps_h[:, a * 512 + 256:a * 512 + 512], gains[:, ds(g + GT, 1)], part,
                                        ALU.mult, ALU.mult).then_inc(s["act_done"], 1)

            def split_act(g, a):
                ve.wait_ge(s["a_hi"], g * 2 + a + 1)
                ve.tensor_tensor(alo[:, a * 256:a * 256 + 256], ps_at[a], ahi[:, a * 256:a * 256 + 256].bitcast(f32),
                                 ALU.subtract).then_inc(s["a_lo"], 1)

            def weigh(g):
                ve.wait_ge(s["w2_read"], g * 2 + 3)
                ve.wait_ge(s["y_out"], (g + 1) * 16)
                ve.tensor_scalar(y[:, 512:1024], ps_y[:, 512:1024], gains[:, ds(g, 1)], None, ALU.mult).then_inc(s["y_lo"], 1)

            def tile(g, j):
                gate_up(g, 0)
                gate_up(g, 1)
                split_act(g, 0)
                split_act(g, 1)
                split_x(g + 1)
                weigh(g)

            def last_tile(g, j):
                gate_up(g, 0)
                split_weights(j + 1, 0)
                split_weights(j + 1, 1)
                gate_up(g, 1)
                split_act(g, 0)
                split_act(g, 1)
                split_x(g + 1)
                split_weights(j + 1, 2)
                split_weights(j + 1, 3)
                weigh(g)
                split_weights(j + 1, 4)
                split_weights(j + 1, 5)

            for q in range(GROUPS):
                split_weights(0, q)
            split_x(0)

            def slot_gains():
                ve.wait_ge(s["slots_in"], 16)
                slots3 = slots.bitcast(f32).rearrange("p (t w) -> p t w", w=4)
                ve.tensor_copy(gains[:, SHARED_TILES:GT], slots3[:, :, 1]).then_inc(s["gains_set"], 1)
                ve.tensor_copy(gains[:, GT + SHARED_TILES:2 * GT], slots3[:, :, 2]).then_inc(s["gains_set"], 1)

            expert_loop(ve, tile, last_tile, slot_gains)

        @block.tensor
        def _(pe):
            pe.wait_ge(s["masks"], 7)
            pe.wait_ge(s["consts_in"], 64)

            def linear(v, par, gated, o):
                pe.wait_ge(s["w0_lo"], v + 2)
                pe.wait_ge(s["w0_hi"], v + 1)
                pe.wait_ge(s["gated_lo"], gated)
                pe.wait_ge(s["gated_hi"], gated)
                pe.wait_ge(s["x1_pre"], v + 1)
                for c in range(CB):
                    for wpart, cpart in ((w0hi, C0HI), (w0hi, C0LO), (w0lo, C0HI)):
                        first = wpart is w0hi and cpart == C0HI and c == 0
                        final = wpart is w0lo and c == CB - 1
                        for h in range(2):
                            last = pe.matmul(ps_x1[:, h * 512:h * 512 + 512], wpart[:, c * P:(c + 1) * P],
                                             halves[:, ds(par * PAR + (cpart + c * SEQ + h * 512), 512)],
                                             start=first, stop=final)
                last.then_inc(s["ffn_done"], 1)
                pe.wait_ge(s["res"], v + 1)
                pe.wait_ge(s["r_copy"], v + 1)
                for t in range(ST):
                    last = pe.transpose(ps_r[:, t * P:(t + 1) * P], XL[:, t * P:(t + 1) * P], ident[:, :])
                last.then_inc(s["r_tr"], 1)
                pe.wait_ge(s["z"], v + 1)
                pe.wait_ge(s["z_copy"], v + 1)
                for t in range(ST):
                    last = pe.transpose(ps_z[:, t * P:(t + 1) * P], C1[:, t * P:(t + 1) * P], ident[:, :])
                last.then_inc(s["z_tr"], 1)
                pe.wait_ge(s["sq"], v + 1)
                pe.wait_ge(s["l_acc"], v + 1)
                for t in range(ST):
                    pe.matmul(ps_l[:, t * 33:t * 33 + 32], C1[:, t * P:(t + 1) * P], rw[:, ds(o * EXPERTS, EXPERTS)],
                              start=True, stop=True)
                    last = pe.matmul(ps_l[:, t * 33 + 32:t * 33 + 33], RL[:, t * P:(t + 1) * P], ones[:, :],
                                     start=True, stop=True)
                last.then_inc(s["l_mm"], 1)

            with pe.Fori(1, BATCH) as b:
                with pe.Fori(0, CB) as c:
                    linear(b * CB + c - CB, (b + 1) % 2, b * CB, c)
            with pe.Fori(0, CB) as c:
                linear(c + (BATCH - 1) * CB, (BATCH - 1) % 2, BLOCKS, c)

            pe.wait_ge(s["rt_mask"], 3)
            pe.wait_ge(s["z_copy"], BLOCKS + 1)
            for h in range(2):
                pe.matmul(ps_x1[:, h * 512:h * 512 + 512], before[:, :], chosen[:, h * 512:h * 512 + 512], start=True, stop=True)
            for h in range(2):
                last = pe.matmul(ps_z[:, h * 512:h * 512 + 512], allb[:, :], chosen[:, h * 512:h * 512 + 512], start=True, stop=True)
            last.then_inc(s["rt_pe"], 1)

            def transpose_x(g):
                pe.wait_ge(s["rows_in"], (g + 1) * 16)
                pe.wait_ge(s["x_lo"], g + 1)
                for c in range(CB):
                    last = pe.transpose(ps_xt[:, c * P:(c + 1) * P], hx[:, c * P:(c + 1) * P], ident[:, :])
                last.then_inc(s["x_tr"], 1)

            def transpose_act(g, a):
                pe.wait_ge(s["act_done"], g * 2 + a + 2)
                for i in range(2):
                    at = a * 256 + i * P
                    last = pe.transpose(ps_at[a][:, i * P:(i + 1) * P], act[:, at:at + P], ident[:, :])
                last.then_inc(s["a_tr"], 1)

            def tile(g, j):
                pe.wait_ge(s["x_lo"], g + 2)
                pe.wait_ge(s["act_done"], g * 2 + 1)
                for q in range(4):
                    a, kh = q // 2, q % 2
                    pe.wait_ge(s["w_lo"], j * GROUPS + q + 2)
                    for k in range(4):
                        xk = kh * 4 + k
                        rhs = slice(q * GC + k * 512, q * GC + k * 512 + 512)
                        for xp, wp in ((xhi, whi), (xhi, wlo), (xlo, whi)):
                            last = pe.matmul(ps_h[:, a * 512:a * 512 + 512], xp[:, xk * P:(xk + 1) * P], wp[:, rhs],
                                             start=(xk == 0 and xp is xhi and wp is whi), stop=(xk == 7 and xp is xlo))
                    last.then_inc(s["w1_read"], 1)
                transpose_act(g, 0)
                transpose_x(g + 1)
                transpose_act(g, 1)
                pe.wait_ge(s["y_lo"], g + 1)
                pe.wait_ge(s["y_hi"], g + 1)
                for q in range(2):
                    pe.wait_ge(s["w_lo"], j * GROUPS + q + 5 + 1)
                    pe.wait_ge(s["a_lo"], g * 2 + q + 1)
                    for k in range(2):
                        for ap_, wp in ((ahi, whi), (ahi, wlo), (alo, whi)):
                            for h in range(2):
                                rhs = (4 + q) * GC + k * 1024 + h * 512
                                last = pe.matmul(ps_y[:, h * 512:h * 512 + 512], ap_[:, (q * 2 + k) * P:(q * 2 + k + 1) * P],
                                                 wp[:, rhs:rhs + 512], start=(q == 0 and k == 0 and ap_ is ahi and wp is whi),
                                                 stop=(q == 1 and k == 1 and ap_ is alo))
                    last.then_inc(s["w2_read"], 1)

            transpose_x(0)
            expert_loop(pe, tile, tile)


def kernel(x, fside_BxSxS_0, cond_512, L0_cond_w, L0_cond_u, L0_ffn_weight, L0_ffn_scale_weight, L0_ffn_bias,
           L1_cond_w, L1_cond_u, L1_ffn_norm_w, L1_ffn_router_w, L1_ffn_w1, L1_ffn_w2, L1_ffn_sg, L1_ffn_su, L1_ffn_sd):
    import numpy as np
    import concourse.bacc as bacc
    from concourse.bass_utils import run_bass_kernel_spmd

    a = lambda v: np.asarray(v)
    by_partition = lambda v: a(v).reshape(CB, P).T
    blocks = lambda v: np.ascontiguousarray(a(v).transpose(0, 2, 1)).reshape(BLOCKS * P, SEQ)
    up = a(L1_ffn_w1)
    halves = lambda v: [v[:, i * INNER:(i + 1) * INNER] for i in range(SHARED)]
    shared_w1 = [np.concatenate(p, 1) for p in zip(halves(a(L1_ffn_sg)), halves(a(L1_ffn_su)))]
    w1 = np.concatenate([np.stack(shared_w1), up])
    w1 = w1.reshape(-1, 2, 4, P, 2, 2, 256).transpose(0, 5, 1, 3, 2, 4, 6).reshape(-1, 4, P, GC)
    w2 = np.concatenate([a(L1_ffn_sd).reshape(SHARED, INNER, CH), a(L1_ffn_w2)])
    w2 = w2.reshape(-1, 2, 2, P, CH).transpose(0, 1, 3, 2, 4).reshape(-1, 2, P, GC)
    expert_w = np.concatenate([w1, w2], 1).reshape(-1, GC)
    arrays = {
        "x_t": blocks(x),
        "side_t": blocks(fside_BxSxS_0),
        "cond": a(cond_512).reshape(1, -1),
        "w_u": np.stack([np.concatenate([by_partition(L0_cond_w), by_partition(L1_cond_w)], 1),
                         np.concatenate([by_partition(L0_cond_u), by_partition(L1_cond_u)], 1)]),
        "lin_w": a(L0_ffn_weight).reshape(CB, P, CB, P).transpose(0, 3, 2, 1).reshape(CB * P, CH),
        "lin_sb": np.concatenate([by_partition(L0_ffn_scale_weight), by_partition(L0_ffn_bias)], 1),
        "norm_w": by_partition(L1_ffn_norm_w),
        "router_t": a(L1_ffn_router_w).reshape(EXPERTS, CB, P).transpose(2, 1, 0).reshape(P, CB * EXPERTS),
        "expert_w": expert_w,
    }
    arrays = {k: np.ascontiguousarray(v) for k, v in arrays.items()}
    nc = bacc.Bacc("TRN2", target_bir_lowering=False, num_devices=1)
    ins = [nc.dram_tensor(k, v.shape, mybir.dt.from_np(v.dtype), kind="ExternalInput").ap() for k, v in arrays.items()]
    out = nc.dram_tensor("out", (TOK + P, CH), mybir.dt.float32, kind="ExternalOutput").ap()
    adaln_moe(nc, *ins, out)
    r = run_bass_kernel_spmd(nc, [arrays], core_ids=[0])
    return r.results[0]["out"][:TOK].reshape(BATCH, SEQ, CH)
```

```python
import concourse.bass as bass
from concourse import mybir
from contextlib import ExitStack
import numpy as np

BATCH, SEQ, CH, COND = 4, 1024, 1024, 256
EXPERTS, TOPK, INNER = 32, 4, 512
SHARED = 1024
P = 128
CB = CH // P
TOK = BATCH * SEQ
TT = TOK // P
BLOCKS = BATCH * CB
HALF = SEQ // 2
HT = HALF // P
HALVES = TOK // HALF
PIECE = CB * P
FILLS_PER_UNIT = 8
UNITS_PER_HALF = BLOCKS // HALVES
STEPS = FILLS_PER_UNIT * UNITS_PER_HALF
ROUTED_TILES = TOK * TOPK // P + EXPERTS
SLOT_TILES = ROUTED_TILES + 2
PUT_FILLS = 2
PUTS = 4
GROUPS = 6
GC = CB * 2 * INNER // 4

def step_l(o):
    return 0 if o == 0 else 2 * o - 1


def step_d(o):
    return 2 * o + 2 if o < CB - 1 else 2 * CB - 1


def step_g(j):
    return 2 * CB + 2 * j


L_AT = {step_l(o): o for o in range(CB)}
FIRST_RANK = 2 * CB + 5
D_AT = {step_d(o): o for o in range(CB)}


def adaln_moe(nc, x_t, side_t, cond, w_all, u_all, lin_sb, norm_w, router_t, shared_w, expert_w, out):
    f32, f32r, bf16 = mybir.dt.float32, mybir.dt.float32r, mybir.dt.bfloat16
    i32, u32 = mybir.dt.int32, mybir.dt.uint32
    ALU, ACT, AX = mybir.AluOpType, mybir.ActivationFunctionType, mybir.AxisListType
    ds = bass.ds

    ratio_dram = nc.dram_tensor("ratio_dram", (BLOCKS * P, SEQ), f32).ap()
    gated_dram = nc.dram_tensor("gated_dram", (BLOCKS * P, SEQ), f32).ap()
    rows_dram = nc.dram_tensor("rows_dram", (TOK + P, CH), f32).ap()
    slots_dram = nc.dram_tensor("slots_dram", (SLOT_TILES * P, 4), i32).ap()

    ctx = ExitStack()
    with ctx:
        def sb(name, cols, dt=f32):
            return ctx.enter_context(nc.sbuf_tensor(name, [P, cols], dt))

        def sem(name):
            return ctx.enter_context(nc.semaphore(name))

        OP = CB * HALF
        halves = sb("halves", 6 * OP + 4 * PIECE, f32r)
        chi, clo, zhi, zlo, ahi_s, alo_s = (halves[:, i * OP:(i + 1) * OP] for i in range(6))
        piece_hi, piece_lo = ([halves[:, 6 * OP + (2 * i + part) * PIECE:6 * OP + (2 * i + part + 1) * PIECE]
                               for i in range(2)] for part in range(2))
        EW = GROUPS * GC
        whi, wlo = halves[:, 0:EW], halves[:, EW:2 * EW]
        xhi, xlo = halves[:, 2 * EW:2 * EW + 1024], halves[:, 2 * EW + 1024:2 * EW + 2048]
        ahi, alo = halves[:, 2 * EW + 2048:2 * EW + 2560], halves[:, 2 * EW + 2560:2 * EW + 3072]

        SCAN = 9 * SEQ
        work = sb("work", SCAN + 2 * PIECE + OP + 13 * HALF)
        K, X, EK, EKV, W, F, G, H, N = (work[:, i * SEQ:(i + 1) * SEQ] for i in range(9))
        piece_in = [work[:, SCAN + i * PIECE:SCAN + (i + 1) * PIECE] for i in range(2)]
        RES = work[:, SCAN + 2 * PIECE:SCAN + 2 * PIECE + OP]
        part0 = SCAN + 2 * PIECE + OP
        XL0, XL1, C10, C11, RL, Z, SQ, ZS, RS, OV, R, T, SG = (
            work[:, part0 + i * HALF:part0 + (i + 1) * HALF] for i in range(13))
        XL, C1 = [XL0, XL1], [C10, C11]

        stage = work[:, 0:EW]
        hx = work[:, EW:EW + 1024]
        y = work[:, EW + 1024:EW + 2048]
        act = work[:, EW + 2048:EW + 2560]
        entry = work[:, part0:part0 + TT * TOPK * 4].bitcast(i32)
        where = work[:, part0 + HALF:part0 + HALF + TT * TOPK].bitcast(i32)
        slots = work[:, part0 + 2 * HALF:part0 + 2 * HALF + 4 * SLOT_TILES].bitcast(i32)

        RESET, LG, CAND, INCL = K, X, EK, H
        HOT = [EKV, W, F, G]
        chosen = N[:, 0:512].bitcast(bf16)
        small, rampf, rev, ramp128, ends = (N[:, 512 + i * 32:512 + (i + 1) * 32] for i in range(5))
        tops = N[:, 768:768 + TOPK * TT]
        EXP30 = float(np.exp(np.float32(30.0)))

        acc = sb("acc", TT * 33)
        rms = sb("rms", TT)
        GT = SLOT_TILES
        gains = acc[:, 0:2 * GT]
        decay = sb("decay", 2 * BLOCKS)
        uu = sb("uu", 2 * BLOCKS)
        ww = sb("ww", 2 * CB)
        lsb = sb("lsb", 2 * CB)
        nrm = sb("nrm", CB)
        rw = sb("rw", CB * EXPERTS)
        ident = sb("ident", P)
        ones = sb("ones", P)
        before = sb("before", P, bf16)
        allb = sb("allb", P, bf16)
        tf = sb("tf", BATCH)
        half_tf = sb("half_tf", BATCH)
        neg_gain = sb("neg_gain", BLOCKS)
        bounds = sb("bounds", EXPERTS + 1, i32)
        finals = sb("finals", EXPERTS, i32)
        row_idx = sb("row_idx", 1, i32)
        add_idx = sb("add_idx", 1, i32)
        ramp = sb("ramp", EXPERTS, i32)
        lsb_neg = sb("lsb_neg", CB)
        put_idx = sb("put_idx", PUTS * TOPK, i32)
        put_val = sb("put_val", PUTS * TOPK * 4, i32)

        ps = [ctx.enter_context(nc.psum_tensor(f"ps{i}", [P, 1024], f32)) for i in range(4)]
        bank = lambda i: ps[i // 2][:, (i % 2) * 512:(i % 2) * 512 + 512]
        Z_BANK, OUT_BANK, SUM_BANK, LOGIT_BANK = (bank(i) for i in range(4, 8))
        ps_cnt = ps[3]
        ps_h, ps_xt, ps_y = ps[0], ps[1], ps[2]
        ps_at = [ps[3][:, 0:256], ps[3][:, 512:768]]

        s = {}
        for name in (
            "k_in x_in ramp consts_in cond_in kc ek ekv euk w_diff h_fwd h_bwd h_sum h_all den g_ln g_inv nf nb "
            "n_sum wv_done num newton1 newton2 sig_steps sig_x gated gated_raw ratio ratio_out gated_out "
            "piece_hi piece_lo product read_out rl_in cl_in c_hi c_lo sig1_steps sig1 c1 z sq z_hi z_lo res "
            "z_tr sums z_copy z_out mean r_ln r_exp newton_r r_set scaled l_tr l_acc silu_steps silu_sig g_r "
            "g_silu a_hi_s a_lo_s o_tr o_copy o_out prep prep_act masks rt rt_act rt_mask rt_pe cnt_copy "
            "fill_set add_idx_set apart entry_ready put_set slots_in gains_set w_hi w_lo w1_read w2_read "
            "rows_in row_idx_set x_tr x_hi x_lo silu_done act_done a_tr a_hi a_lo y_hi y_lo y_out zero_set "
            "zero_out"
        ).split():
            s[name] = sem(name)

        ONE_AHEAD = (
            "o_tr o_copy o_out gated w_lo num ratio_out gated_out a_tr w1_read w2_read act_done x_lo y_lo y_hi"
        ).split()
        piece_sem = [sem(f"piece_in{i}") for i in range(2)]
        put_sem = [sem(f"put_out{i}") for i in range(PUTS)]
        puts_before = lambda q: 16 if q < PUT_FILLS else 0
        xl_sem = [sem(f"xl_in{i}") for i in range(2)]
        w_in = [sem(f"w_in{q}") for q in range(GROUPS)]
        block = ctx.enter_context(nc.Block())

        def apart(eng):
            eng.sem_inc(s["apart"], 1)

        def wait(eng, name, value):
            if not (isinstance(value, int) and value <= 0):
                eng.wait_ge(s[name], value)

        def before_all(h):
            return isinstance(h, int) and h < 0

        def final(h, which=HALVES - 1):
            return isinstance(h, int) and h == which

        def number(step, first):
            return L_AT[step] if first and step < 2 * CB else step - CB

        def products(h, first):
            return [(i, number(i, first)) for i in range(STEPS) if not (first and i in D_AT)]

        def x_added(h, o, first):
            return h * STEPS + (number(step_l(o), first) + 1)

        def summed(h, o):
            return (h + 1) * STEPS + ((o if final(h) else step_d(o)) - CB + 1)

        def scaled_gate(h, j):
            return h * STEPS + (CB + 2 * j + 1)

        def half_rows(h, o):
            return ds((h // 2 * CB + o) * P, P), ds(h % 2 * HALF, HALF)

        def split_piece_lo(eng, h, k):
            eng.wait_ge(s["piece_hi"], h * STEPS + (k + 1))
            eng.tensor_tensor(piece_lo[k % 2], piece_in[k % 2], piece_hi[k % 2].bitcast(f32),
                               ALU.subtract).then_inc(s["piece_lo"], 1)

        def gate_r(eng, h, j):
            eng.wait_ge(s["silu_steps"], (h * CB + j) * 2 + 1)
            eng.tensor_tensor(T, T, R, ALU.mult).then_inc(s["g_r"], 1)

        def gate_silu(eng, h, j):
            eng.wait_ge(s["silu_sig"], h * CB + (j + 1))
            eng.wait_ge(s["g_r"], h * CB + (j + 1))
            eng.tensor_tensor(T, T, SG, ALU.mult).then_inc(s["g_silu"], 1)

        def split_act_lo(eng, h, j):
            eng.wait_ge(s["a_hi_s"], h * CB + (j + 1))
            part = slice(j * HALF, (j + 1) * HALF)
            eng.tensor_tensor(alo_s[:, part], OV, ahi_s[:, part].bitcast(f32), ALU.subtract).then_inc(s["a_lo_s"], 1)

        def low_halves(eng, h, i, first, prev, next_):
            if prev and i == 0:
                gate_r(eng, h - 1, CB - 1)
                gate_silu(eng, h - 1, CB - 1)
            if prev and i == 1:
                split_act_lo(eng, h - 1, CB - 1)
            if not before_all(h):
                if any(i == a for a, _ in products(h, first)):
                    split_piece_lo(eng, h, number(i, first) + 1)
                for o in range(CB):
                    if i == step_l(o) + 3:
                        eng.wait_ge(s["z_hi"], h * CB + (o + 1))
                        part = slice(o * HALF, (o + 1) * HALF)
                        eng.tensor_tensor(zlo[:, part], Z, zhi[:, part].bitcast(f32), ALU.subtract).then_inc(s["z_lo"], 1)
                for j in range(CB - 1):
                    if i == step_g(j) + 2:
                        gate_r(eng, h, j)
                        gate_silu(eng, h, j)
                    if i == step_g(j) + 3:
                        split_act_lo(eng, h, j)
            if next_:
                for c in range(CB):
                    if i == STEPS - CB + c:
                        eng.wait_ge(s["c_hi"], (h + 1) * CB + (c + 1))
                        part = slice(c * HALF, (c + 1) * HALF)
                        eng.tensor_tensor(clo[:, part], RL, chi[:, part].bitcast(f32), ALU.subtract).then_inc(s["c_lo"], 1)

        def expert_loop(eng, tile, last_tile):
            eng.wait_ge(s["gains_set"], 2)

            def group(e, last_tile):
                first = eng.value_load(bounds[0:1, ds(e, 1)], min_val=0, max_val=ROUTED_TILES)
                final = eng.value_load(finals[0:1, ds(e, 1)], min_val=0, max_val=ROUTED_TILES - 1)
                with eng.If(first < final):
                    with eng.Fori(first, final) as g:
                        tile(g, e)
                last_tile(final, e)

            with eng.Fori(0, EXPERTS - 1) as e:
                group(e, last_tile)
            group(EXPERTS - 1, tile)

        def with_halves(eng, unit, fill, tail):
            nothing = lambda i: None
            with eng.Fori(0, 2 * UNITS_PER_HALF - 1) as u:
                unit(u, nothing, alone=True)
            unit(2 * UNITS_PER_HALF - 1, lambda i: fill(-1, STEPS - FILLS_PER_UNIT + i, first=False, prev=False, next_=True))
            for q in range(UNITS_PER_HALF):
                unit(2 * UNITS_PER_HALF + q, lambda i: fill(0, q * FILLS_PER_UNIT + i, first=True, prev=False, next_=True))
            with eng.Fori(1, HALVES - 2) as h:
                for q in range(UNITS_PER_HALF):
                    unit(h * UNITS_PER_HALF + (2 * UNITS_PER_HALF + q),
                         lambda i: fill(h, q * FILLS_PER_UNIT + i, first=False, prev=True, next_=True))
            for h in range(HALVES - 2, HALVES):
                for i in range(STEPS):
                    fill(h, i, first=False, prev=True, next_=h < HALVES - 1)
            tail()

        @block.sync
        def _(sp):
            for name in ONE_AHEAD:
                sp.sem_inc(s[name], 1)
            sp.dma_start(ww[:, :], w_all).then_inc(s["cond_in"], 16)
            sp.dma_start(work[:, 0:BATCH * COND], cond.to_broadcast([P, BATCH * COND])).then_inc(s["cond_in"], 16)
            for dst, src in ((uu, u_all), (lsb, lin_sb), (nrm, norm_w), (rw, router_t)):
                sp.dma_start(dst[:, :], src).then_inc(s["consts_in"], 16)

            def load_side(u):
                wait(sp, "wv_done", 2 * u)
                sp.dma_start(K, side_t[ds(u % BLOCKS * P, P), :]).then_inc(s["k_in"], 16)

            def load_x(u):
                sp.wait_ge(s["gated"], u + 1)
                sp.dma_start(X, x_t[ds(u % BLOCKS * P, P), :]).then_inc(s["x_in"], 16)

            def load_piece(h, k, src):
                wait(sp, "piece_lo", h * STEPS + (k - 1))
                sp.dma_start(piece_in[k % 2], src).then_inc(piece_sem[k % 2], 16)

            w_of = lambda step: shared_w[step * P:(step + 1) * P, :]
            first_half = [(k, w_of(i)) for i, k in products(0, True)]
            other = [(k, w_of(i)) for i, k in products(1, False)]

            def fill(h, i, first, prev, next_):
                if not before_all(h) and any(i == a for a, _ in products(h, first)):
                    k = number(i, first)
                    ahead = k + 2
                    seq = dict(first_half if first else other)
                    if ahead in seq:
                        load_piece(h, ahead, seq[ahead])
                    elif next_:
                        load_piece(h, ahead, w_of(ahead - (STEPS - CB)))
                    else:
                        load_piece(h, ahead, w_of(step_d(ahead - (STEPS - CB))))
                if not before_all(h):
                    for o in range(CB):
                        rows, cols = half_rows(h, o)
                        if i == step_l(o):
                            wait(sp, "res", h * CB + (o - 1))
                            sp.dma_start(XL[o % 2], x_t[rows, cols]).then_inc(xl_sem[o % 2], 16)
                        if i == (2 if o == 1 else step_l(o)):
                            wait(sp, "c1", h * CB + o)
                            sp.wait_ge(s["c_lo"], (h + 1) * CB)
                            if o == 0:
                                sp.wait_ge(s["ratio_out"], (h // 2 + 1) * CB * 16 + 1)
                            sp.dma_start(RL, ratio_dram[rows, cols]).then_inc(s["rl_in"], 16)
                        if i == step_l(o) + 4:
                            sp.wait_ge(s["z_copy"], h * CB + (o + 1))
                            to = rows_dram[ds(h * HALF, HALF), o * P:(o + 1) * P].rearrange("(t p) c -> p t c", p=P)
                            sp.dma_start(to, ZS.rearrange("p (t c) -> p t c", c=P)).then_inc(s["z_out"], 16)
                        if prev and i == step_d(o) + 3:
                            store_out(h - 1, o)
                if final(h, HALVES - 2) and i == 2:
                    store_zeros()
                if next_:
                    for c in range(CB):
                        if i == STEPS - CB + c:
                            rows, cols = half_rows(h + 1, c)
                            if c == 0:
                                wait(sp, "c1", h * CB + CB)
                            wait(sp, "c_lo", (h + 1) * CB + c)
                            sp.wait_ge(s["gated_out"], (((h + 1) // 2) * CB + (c + 1)) * 16 + 1)
                            sp.dma_start(RL, gated_dram[rows, cols]).then_inc(s["cl_in"], 16)

            def store_zeros():
                sp.wait_ge(s["zero_set"], 1)
                sp.dma_start(rows_dram[TOK:TOK + P, :], K).then_inc(s["zero_out"], 16)

            def store_out(h, o):
                sp.wait_ge(s["o_copy"], h * CB + (o + 2))
                to = out[ds(h * HALF, HALF), o * P:(o + 1) * P].rearrange("(t p) c -> p t c", p=P)
                sp.dma_start(to, RS.rearrange("p (t c) -> p t c", c=P)).then_inc(s["o_out"], 16)

            def unit(u, fill, alone=False):
                fill(0)
                fill(1)
                fill(2)
                fill(3)
                sp.wait_ge(s["gated"], u + 2)
                sp.dma_start(gated_dram[ds(u * P, P), :], N).then_inc(s["gated_out"], 16)
                load_x(u + 1)
                fill(4)
                fill(5)
                load_side(u + 1)
                fill(6)
                fill(7)
                sp.wait_ge(s["ratio"], u + 1)
                sp.dma_start(ratio_dram[ds(u * P, P), :], N).then_inc(s["ratio_out"], 16)

            def tail():
                for o in range(CB):
                    if o + 2 < CB:
                        load_piece(HALVES, o + 2 - CB, w_of(step_d(o + 2)))
                    if o:
                        store_out(HALVES - 1, o - 1)
                store_out(HALVES - 1, CB - 1)

            sp.wait_ge(s["prep"], 1)
            load_side(0)
            load_x(0)
            for k, src in first_half[:2]:
                load_piece(0, k, src)
            with_halves(sp, unit, fill, tail)

            def load_weights(j):
                for q in range(GROUPS):
                    sp.wait_ge(s["w_lo"], j * GROUPS + q - (GROUPS - 2))
                    sp.dma_start(stage[:, q * GC:(q + 1) * GC],
                                 expert_w[ds((j * GROUPS + q) * P, P), :]).then_inc(w_in[q], 16)

            sp.wait_ge(s["entry_ready"], 1)
            sp.wait_ge(s["read_out"], HALVES * STEPS)
            sp.wait_ge(s["piece_lo"], HALVES * STEPS)
            for q in range(GROUPS):
                sp.dma_start(stage[:, q * GC:(q + 1) * GC], expert_w[q * P:(q + 1) * P, :]).then_inc(w_in[q], 16)
            load_weights(1)
            for q in range(PUTS):
                sp.wait_ge(put_sem[q], 16 * (TT // PUTS * TOPK) + puts_before(q))
            sp.dma_start(slots.rearrange("p (t w) -> p t w", w=4),
                         slots_dram.rearrange("(t p) w -> p t w", p=P)).then_inc(s["slots_in"], 16)
            with sp.Fori(2, EXPERTS) as j:
                load_weights(j)

        @block.gpsimd
        def _(pool):
            pool.memset(ident[:, :], 0.0).then_inc(s["masks"], 1)
            pool.memset(allb[:, :], 1.0).then_inc(s["masks"], 1)
            pool.memset(before[:, :], 1.0).then_inc(s["masks"], 1)
            pool.memset(ones[:, :], 1.0).then_inc(s["masks"], 1)
            pool.wait_ge(s["masks"], 4)
            pool.affine_select(out=ident[:, :], in_=ident[:, :], compare_op=ALU.not_equal, fill=1.0,
                               base=0, pattern=[[-1, P]], channel_multiplier=1).then_inc(s["masks"], 1)
            pool.affine_select(out=before[:, :], in_=before[:, :], compare_op=ALU.is_gt, fill=0.0,
                               base=0, pattern=[[1, P]], channel_multiplier=-1).then_inc(s["masks"], 1)
            pool.iota(ramp[:, :], pattern=[[1, EXPERTS]], base=0, channel_multiplier=0).then_inc(s["ramp"], 1)

            def gather_rows(g):
                pool.tensor_copy(row_idx[:, :], slots[:, ds(g * 4, 1)]).then_inc(s["row_idx_set"], 1)
                pool.wait_ge(s["row_idx_set"], g + 1)
                apart(pool)
                pool.indirect_dma_start(hx, None, rows_dram[:, :],
                                        bass.IndirectOffsetOnAxis(row_idx[:, :].bitcast(u32), 0)).then_inc(s["rows_in"], 16)

            def await_y(g):
                pool.wait_ge(s["y_hi"], g + 2)
                pool.wait_ge(s["y_lo"], g + 2)
                pool.wait_ge(s["y_out"], 16 * (g + 1))

            def put_entries(t, par):
                idx, val = put_idx[:, par * TOPK:(par + 1) * TOPK], put_val[:, par * TOPK * 4:(par + 1) * TOPK * 4]
                done_before = t * (16 * TOPK) + puts_before(par)
                if not isinstance(done_before, int) or done_before:
                    pool.wait_ge(put_sem[par], done_before)
                t = t * PUTS + par
                pool.tensor_copy(idx, where[:, ds(t * TOPK, TOPK)]).then_inc(s["put_set"], 1)
                pool.tensor_copy(val, entry[:, ds(t * TOPK * 4, TOPK * 4)]).then_inc(s["put_set"], 1)
                pool.wait_ge(s["put_set"], 2 * t + 2)
                for k in range(TOPK):
                    apart(pool)
                    pool.indirect_dma_start(slots_dram[:, :], bass.IndirectOffsetOnAxis(idx[:, k:k + 1].bitcast(u32), 0),
                                            val[:, 4 * k:4 * k + 4], None).then_inc(put_sem[par], 16)

            def empty_slots():
                pool.wait_ge(s["res"], HALVES * CB)
                pool.iota(entry.rearrange("p (t k w) -> p t k w", k=TOPK, w=4)[:, :, :, 0],
                          pattern=[[P, TT], [0, TOPK]], base=0, channel_multiplier=1).then_inc(s["ramp"], 1)
                pool.memset(slots, 0).then_inc(s["fill_set"], 1)
                pool.wait_ge(s["fill_set"], 1)
                pool.iota(slots.rearrange("p (t w) -> p t w", w=4)[:, :, 0], pattern=[[0, SLOT_TILES]],
                          base=TOK, channel_multiplier=1).then_inc(s["fill_set"], 1)
                pool.wait_ge(s["fill_set"], 2)
                for q in range(PUT_FILLS):
                    n = SLOT_TILES // PUT_FILLS
                    pool.dma_start(slots_dram[q * n * P:(q + 1) * n * P, :].rearrange("(t p) w -> p t w", p=P),
                                   slots[:, 4 * q * n:4 * (q + 1) * n].rearrange("p (t w) -> p t w", w=4))\
                        .then_inc(put_sem[q], 16)

            def fill(h, i, first, prev, next_):
                if final(h) and i == FIRST_RANK + 1:
                    empty_slots()
                if final(h, HALVES - 2) and i == 2:
                    pool.wait_ge(s["zero_set"], 1)
                    pool.dma_start(out[TOK:TOK + P, :], K).then_inc(s["y_out"], 16)
                if not final(h) or i <= FIRST_RANK:
                    low_halves(pool, h, i, first, prev, next_)

            def unit(u, fill, alone=False):
                for i in range(FILLS_PER_UNIT):
                    fill(i)
                if alone:
                    pool.wait_ge(s["ek"], u + 1)
                    pool.tensor_tensor(EKV, EK, K, ALU.mult).then_inc(s["ekv"], 1)
                    for l in range(2):
                        pool.wait_ge(s["h_all"], u * 2 + l + 1)
                        pool.tensor_tensor(W, W, K, ALU.mult).then_inc(s["wv_done"], 1)

            split_piece_lo(pool, 0, 0)
            with_halves(pool, unit, fill, lambda: None)
            pool.wait_ge(s["entry_ready"], 1)
            for q in range(PUT_FILLS):
                pool.wait_ge(put_sem[q], 16)
            for par in range(PUTS):
                put_entries(0, par)
            with pool.Fori(1, TT // PUTS) as t:
                for par in range(PUTS):
                    put_entries(t, par)
            pool.wait_ge(s["zero_out"], 16)
            pool.wait_ge(s["z_out"], 16 * HALVES * CB)
            pool.wait_ge(s["o_out"], 16 * HALVES * CB + 1)
            pool.wait_ge(s["slots_in"], 16)
            gather_rows(0)
            pool.wait_ge(s["x_tr"], 1)
            gather_rows(1)
            tiles = pool.value_load(bounds[0:1, EXPERTS:EXPERTS + 1], min_val=EXPERTS, max_val=ROUTED_TILES)
            with pool.Fori(0, tiles) as g:
                pool.wait_ge(s["x_tr"], g + 2)
                gather_rows(g + 2)
                await_y(g)
                pool.tensor_copy(add_idx[:, :], slots[:, ds(g * 4, 1)]).then_inc(s["add_idx_set"], 1)
                pool.wait_ge(s["add_idx_set"], g + 1)
                apart(pool)
                pool.indirect_dma_start(out[:, :], bass.IndirectOffsetOnAxis(add_idx[:, :].bitcast(u32), 0),
                                        y, None, compute_op=ALU.add).then_inc(s["y_out"], 16)
            pool.wait_ge(s["rows_in"], (tiles + 2) * 16)
            pool.wait_ge(s["y_out"], (tiles + 1) * 16)

        @block.scalar
        def _(sc):
            sc.wait_ge(s["prep"], 1)
            sc.activation(tf[:, :], tf[:, :], ACT.Sigmoid).then_inc(s["prep_act"], 1)
            sc.wait_ge(s["cond_in"], 32)
            sc.activation(ww[:, :], ww[:, :], ACT.Exp).then_inc(s["prep_act"], 1)
            sc.wait_ge(s["prep_act"], 2)
            sc.activation(ww[:, :], ww[:, :], ACT.Exp, scale=-1.0).then_inc(s["prep_act"], 1)

            def sigmoid(place, src, steps, n, out_sem, bias=0.0):
                sc.activation(place, src, ACT.Exp, scale=-1.0, bias=bias).then_inc(s[steps], 1)
                sc.wait_ge(s[steps], n * 2 + 1)
                sc.activation(place, place, ACT.Ln, bias=ones[:, 0:1]).then_inc(s[steps], 1)
                sc.wait_ge(s[steps], n * 2 + 2)
                sc.activation(place, place, ACT.Exp, scale=-1.0).then_inc(s[out_sem], 1)

            def side_exp(u):
                sc.wait_ge(s["kc"], u + 1)
                sc.activation(EK, EK, ACT.Exp).then_inc(s["ek"], 1)

            def unit(u, fill, alone=False):
                fill(0)

                def euk(l):
                    sc.wait_ge(s["num"], u * 2 + l + 1)
                    apart(sc)
                    sc.activation(W, K, ACT.Exp, bias=uu[:, ds(u + l * BLOCKS, 1)]).then_inc(s["euk"], 1)

                def inverse(l):
                    sc.wait_ge(s["den"], u * 2 + l + 1)
                    sc.activation(G, H, ACT.Ln).then_inc(s["g_ln"], 1)
                    sc.wait_ge(s["g_ln"], u * 2 + l + 1)
                    sc.activation(G, G, ACT.Exp, scale=-1.0).then_inc(s["g_inv"], 1)

                euk(0)
                sc.wait_ge(s["x_in"], (u + 1) * 16)
                sigmoid(X, X, "sig_steps", u, "sig_x")
                fill(1)
                fill(2)
                inverse(0)
                fill(3)
                euk(1)
                fill(4)
                fill(5)
                fill(6)
                inverse(1)
                fill(7)
                side_exp(u + 1)

            def split_piece(h, k):
                wait(sc, "product", h * STEPS + (k - 1))
                n = (h * (STEPS // 2) + (k // 2 + 1)) * 16
                sc.wait_ge(piece_sem[k % 2], n)
                sc.activation(piece_hi[k % 2], piece_in[k % 2], ACT.Copy).then_inc(s["piece_hi"], 1)

            def silu(h, j):
                sc.wait_ge(s["read_out"], scaled_gate(h, j))
                wait(sc, "g_silu", h * CB + j)
                sigmoid(SG, T, "silu_steps", h * CB + j, "silu_sig")

            def act_hi(h, j):
                sc.wait_ge(s["read_out"], scaled_gate(h, j) + 1)
                if j == 0:
                    wait(sc, "product", h * STEPS + CB)
                sc.activation(ahi_s[:, j * HALF:(j + 1) * HALF], OV, ACT.Copy).then_inc(s["a_hi_s"], 1)

            def out_copy(h, o):
                sc.wait_ge(s["o_tr"], h * CB + (o + 2))
                sc.wait_ge(s["o_out"], (h * CB + o) * 16 + 1)
                sc.activation(RS, OUT_BANK, ACT.Copy).then_inc(s["o_copy"], 1)

            def fill(h, i, first, prev, next_):
                if not before_all(h):
                    if any(i == a for a, _ in products(h, first)):
                        split_piece(h, number(i, first) + 1)
                    for o in range(CB):
                        if prev and i == step_d(o) + 2:
                            out_copy(h - 1, o)
                        if i == step_l(o) + 3:
                            sc.wait_ge(s["z_tr"], h * CB + (o + 1))
                            wait(sc, "z_out", (h * CB + o) * 16)
                            sc.activation(ZS, Z_BANK, ACT.Copy).then_inc(s["z_copy"], 1)
                        if i == step_l(o) + 2:
                            sc.wait_ge(s["z"], h * CB + (o + 1))
                            part = slice(o * HALF, (o + 1) * HALF)
                            if o == 0:
                                wait(sc, "product", h * STEPS - CB)
                            sc.activation(zhi[:, part], Z, ACT.Copy).then_inc(s["z_hi"], 1)
                            wait(sc, "sums", h * CB + o)
                            sc.activation(SQ, C1[o % 2], ACT.Square).then_inc(s["sq"], 1)
                    for o in range(CB):
                        if i == step_l(o) + 1:
                            sc.wait_ge(s["read_out"], x_added(h, o, first))
                            wait(sc, "res", h * CB + (o - 1))
                            sigmoid(C1[o % 2], XL[o % 2], "sig1_steps", h * CB + o, "sig1", bias=lsb_neg[:, o:o + 1])
                    if i == 2 * CB:
                        sc.wait_ge(s["mean"], h + 1)
                        sc.activation(R, SQ, ACT.Ln).then_inc(s["r_ln"], 1)
                        sc.wait_ge(s["r_ln"], h + 1)
                        sc.activation(R, R, ACT.Exp, scale=-0.5).then_inc(s["r_exp"], 1)
                if prev and i == 0:
                    silu(h - 1, CB - 1)
                if prev and i == 1:
                    act_hi(h - 1, CB - 1)
                if not before_all(h):
                    for j in range(CB - 1):
                        if i == step_g(j) + 2:
                            silu(h, j)
                        if i == step_g(j) + 3:
                            act_hi(h, j)
                if next_:
                    for c in range(CB):
                        if i == STEPS - CB + c:
                            sc.wait_ge(s["cl_in"], ((h + 1) * CB + (c + 1)) * 16)
                            if c == 0 and not before_all(h):
                                sc.wait_ge(s["product"], h * STEPS + CB)
                            sc.activation(chi[:, c * HALF:(c + 1) * HALF], RL, ACT.Copy).then_inc(s["c_hi"], 1)
                if final(h) and i == FIRST_RANK:
                    sc.wait_ge(s["rt_mask"], 1)
                    sc.activation(tops, tops, ACT.Exp).then_inc(s["rt_act"], 1)

            def tail():
                silu(HALVES - 1, CB - 1)
                act_hi(HALVES - 1, CB - 1)
                for o in range(CB):
                    if o + 1 < CB:
                        split_piece(HALVES, o + 1 - CB)
                    if o:
                        out_copy(HALVES - 1, o - 1)
                out_copy(HALVES - 1, CB - 1)

            sc.wait_ge(s["consts_in"], 64)
            sc.wait_ge(s["masks"], 4)
            sc.activation(lsb_neg[:, :], lsb[:, CB:2 * CB], ACT.Copy, scale=-1.0).then_inc(s["prep_act"], 1)
            sc.wait_ge(s["prep_act"], 4)
            sc.preload_act_table_set("natural_log_exp_and_others")
            split_piece(0, 0)
            side_exp(0)
            with_halves(sc, unit, fill, tail)

            sc.wait_ge(s["entry_ready"], 1)
            sc.wait_ge(s["product"], HALVES * STEPS)
            sc.wait_ge(s["a_lo_s"], HALVES * CB)
            def split_x(g):
                sc.wait_ge(s["x_tr"], g + 1)
                sc.activation(xhi, ps_xt[:, :], ACT.Copy).then_inc(s["x_hi"], 1)

            def split_weights(j, q, g):
                sc.wait_ge(w_in[q], (j + 1) * 16)
                if g is not None:
                    sc.wait_ge(s["w1_read"] if q < 4 else s["w2_read"], g * 4 + (q - 2) if q < 4 else g * 2 + (q - 4))
                sc.activation(whi[:, q * GC:(q + 1) * GC], stage[:, q * GC:(q + 1) * GC],
                              ACT.Copy).then_inc(s["w_hi"], 1)

            def silu(g, a):
                sc.wait_ge(s["w1_read"], g * 4 + 2 * a + 3)
                sc.wait_ge(s["a_tr"], g * 2 + 1)
                apart(sc)
                sc.activation(act[:, a * 256:a * 256 + 256], ps_h[:, a * 512:a * 512 + 256], ACT.Silu,
                              scale=gains[:, ds(g + GT, 1)]).then_inc(s["silu_done"], 1)

            def split_act(g, a):
                sc.wait_ge(s["a_tr"], g * 2 + a + 2)
                sc.wait_ge(s["w2_read"], g * 2 + 1)
                sc.activation(ahi[:, a * 256:a * 256 + 256], ps_at[a], ACT.Copy).then_inc(s["a_hi"], 1)

            def weigh(g):
                sc.wait_ge(s["w2_read"], g * 2 + 3)
                sc.wait_ge(s["y_out"], (g + 1) * 16)
                apart(sc)
                sc.activation(y[:, 0:512], ps_y[:, 0:512], ACT.Copy, scale=gains[:, ds(g, 1)]).then_inc(s["y_hi"], 1)

            def tile(g, j):
                silu(g, 0)
                silu(g, 1)
                split_act(g, 0)
                split_act(g, 1)
                split_x(g + 1)
                weigh(g)

            def last_tile(g, j):
                silu(g, 0)
                split_weights(j + 1, 0, g + 1)
                split_weights(j + 1, 1, g + 1)
                silu(g, 1)
                split_act(g, 0)
                split_act(g, 1)
                split_x(g + 1)
                split_weights(j + 1, 2, g + 1)
                split_weights(j + 1, 3, g + 1)
                weigh(g)
                split_weights(j + 1, 4, g + 1)
                split_weights(j + 1, 5, g + 1)

            for q in range(GROUPS):
                split_weights(0, q, None)
            split_x(0)
            expert_loop(sc, tile, last_tile)

        @block.vector
        def _(ve):
            ve.wait_ge(s["cond_in"], 32)
            ve.reduce_sum(tf[:, :], work[:, 0:BATCH * COND].rearrange("p (b d) -> p b d", b=BATCH),
                          axis=AX.X).then_inc(s["prep"], 1)
            ve.wait_ge(s["prep_act"], 3)
            ve.tensor_scalar(half_tf[:, :], tf[:, :], 0.5, 0.5, ALU.mult, ALU.add).then_inc(s["prep"], 1)
            for b in range(BATCH):
                ve.tensor_scalar(neg_gain[:, b * CB:(b + 1) * CB], tf[:, b:b + 1].to_broadcast([P, CB]), -0.2, -0.8,
                                 ALU.mult, ALU.add).then_inc(s["prep"], 1)
            ve.wait_ge(s["prep"], 2 + BATCH)
            for l in range(2):
                for b in range(BATCH):
                    ve.tensor_scalar(decay[:, l * BLOCKS + b * CB:l * BLOCKS + (b + 1) * CB], ww[:, l * CB:(l + 1) * CB],
                                     half_tf[:, b:b + 1], None, ALU.mult).then_inc(s["prep"], 1)
            ve.wait_ge(s["prep"], 2 + 3 * BATCH)
            ve.wait_ge(s["consts_in"], 64)

            def clip(u):
                ve.wait_ge(s["k_in"], (u + 1) * 16)
                ve.tensor_scalar(EK, K, 30.0, None, ALU.min).then_inc(s["kc"], 1)

            def unit(u, fill, alone=False):
                fill(0)
                ve.wait_ge(s["ek"], u + 1)
                if not alone:
                    ve.tensor_tensor(EKV, EK, K, ALU.mult).then_inc(s["ekv"], 1)
                for l in range(2):
                    n = u * 2 + l
                    d = decay[:, ds(u + l * BLOCKS, 1)].to_broadcast([P, SEQ])
                    ve.tensor_tensor_scan(H, d, EK, 0.0, ALU.mult, ALU.add).then_inc(s["h_fwd"], 1)
                    ve.tensor_tensor_scan(G[:, ::-1], d, EK[:, ::-1], 0.0, ALU.mult, ALU.add).then_inc(s["h_bwd"], 1)
                    fill(4 * l + 1)
                    ve.wait_ge(s["euk"], n + 1)
                    ve.scalar_tensor_tensor(W, W, EXP30, EK, ALU.min, ALU.subtract).then_inc(s["w_diff"], 1)
                    ve.wait_ge(s["h_bwd"], n + 1)
                    ve.wait_ge(s["h_fwd"], n + 1)
                    ve.tensor_tensor(H, H, G, ALU.add).then_inc(s["h_sum"], 1)
                    ve.wait_ge(s["h_sum"], n + 1)
                    ve.wait_ge(s["w_diff"], n + 1)
                    ve.tensor_tensor(H, H, W, ALU.add).then_inc(s["h_all"], 1)
                    ve.wait_ge(s["h_all"], n + 1)
                    ve.tensor_scalar(H, H, 1e-8, None, ALU.max).then_inc(s["den"], 1)
                    if l == 0:
                        ve.wait_ge(s["ekv"], u + 1)
                    ve.tensor_tensor_scan(F, d, EKV, 0.0, ALU.mult, ALU.add).then_inc(s["nf"], 1)
                    if l == 0:
                        ve.wait_ge(s["ratio_out"], u * 16 + 1)
                    else:
                        ve.wait_ge(s["gated_out"], (u + 1) * 16 + 1)
                    ve.tensor_tensor_scan(N[:, ::-1], d, EKV[:, ::-1], 0.0, ALU.mult, ALU.add).then_inc(s["nb"], 1)
                    fill(4 * l + 2)
                    if not alone:
                        ve.tensor_tensor(W, W, K, ALU.mult).then_inc(s["wv_done"], 1)
                    ve.wait_ge(s["nf"], n + 1)
                    ve.wait_ge(s["nb"], n + 1)
                    ve.tensor_tensor(F, F, N, ALU.add).then_inc(s["n_sum"], 1)
                    ve.wait_ge(s["n_sum"], n + 1)
                    ve.wait_ge(s["wv_done"], n + 1)
                    ve.tensor_tensor(F, F, W, ALU.add).then_inc(s["num"], 1)
                    fill(4 * l + 3)
                    if l == 1:
                        clip(u + 1)
                    ve.wait_ge(s["g_inv"], n + 1)
                    ve.wait_ge(s["den"], n + 1)
                    ve.tensor_tensor(N, H, G, ALU.mult).then_inc(s["newton1"], 1)
                    ve.wait_ge(s["newton1"], n + 1)
                    ve.scalar_tensor_tensor(N, N, 2.0, G, ALU.subtract, ALU.mult).then_inc(s["newton2"], 1)
                    ve.wait_ge(s["newton2"], n + 1)
                    ve.wait_ge(s["num"], n + 2)
                    ve.scalar_tensor_tensor(N, F, neg_gain[:, ds(u, 1)], N, ALU.mult, ALU.mult)\
                        .then_inc(s["gated_raw"] if l == 0 else s["ratio"], 1)
                    if l == 0:
                        ve.wait_ge(s["gated_raw"], u + 1)
                        ve.wait_ge(s["sig_x"], u + 1)
                        ve.tensor_tensor(N, N, X, ALU.mult).then_inc(s["gated"], 1)
                        fill(4)

            steps = [0]

            def done(instruction):
                steps[0] += 1
                instruction.then_inc(s["rt"], 1)
                ve.wait_ge(s["rt"], steps[0])

            te = lambda a: a.rearrange("p (t e) -> p t e", e=EXPERTS)
            per_t = lambda a: a.rearrange("p (t o) -> p t o", o=1).to_broadcast([P, TT, EXPERTS])
            per_e = lambda a: a.rearrange("p (o e) -> p o e", o=1).to_broadcast([P, TT, EXPERTS])
            acc3 = acc[:, :].rearrange("p (t e) -> p t e", e=EXPERTS + 1)
            et = lambda a: a.rearrange("p (e t) -> p e t", t=TT)
            by_te = lambda a: a.rearrange("p (e t) -> p t e", t=TT)
            tops3 = tops.rearrange("p (k t) -> p k t", k=TOPK)
            entry4 = entry.bitcast(f32).rearrange("p (t k w) -> p t k w", k=TOPK, w=4)

            def rank(t0, t1, choices):
                n = t1 - t0
                at = slice(t0 * EXPERTS, t1 * EXPERTS)
                logits, cand, mark = LG[:, at], CAND[:, at], small[:, t0:t1]
                by_t = lambda a: a.rearrange("p (t o) -> p t o", o=1).to_broadcast([P, n, EXPERTS])
                if choices[0] == 0:
                    done(ve.tensor_copy(rms[:, t0:t1], acc3[:, t0:t1, EXPERTS]))
                    done(ve.tensor_copy(te(logits), acc3[:, t0:t1, 0:EXPERTS]))
                for k in choices:
                    top, hot = tops[:, k * TT + t0:k * TT + t1], HOT[k][:, at]
                    done(ve.reduce_max(top, te(logits), axis=AX.X))
                    done(ve.tensor_tensor(te(cand), te(logits), by_t(top), ALU.is_equal))
                    done(ve.tensor_tensor(te(cand), te(cand),
                                          rev.rearrange("p (o e) -> p o e", o=1).to_broadcast([P, n, EXPERTS]), ALU.mult))
                    done(ve.reduce_max(mark, te(cand), axis=AX.X))
                    done(ve.tensor_tensor(te(hot), te(cand), by_t(mark), ALU.is_equal))
                    done(ve.scalar_tensor_tensor(logits, hot, -1e30, logits, ALU.mult, ALU.add))

            def rank_early(portion):
                if portion == 0:
                    ve.wait_ge(s["ratio_out"], 16 * BLOCKS + 1)
                    ve.wait_ge(s["l_acc"], HALVES - 1)
                    done(ve.tensor_copy(rampf, ramp[:, :]))
                    done(ve.tensor_scalar(rev, rampf, -1.0, float(EXPERTS), ALU.mult, ALU.add))
                    done(ve.tensor_scalar(ramp128, rampf, float(P), None, ALU.mult))
                    ve.wait_ge(s["zero_out"], 16)
                    ve.wait_ge(s["y_out"], 16)
                    done(ve.memset(RESET, 1.0))
                    done(ve.memset(et(RESET)[:, :, 0:1], 0.0))
                elif portion % 2 == 0 and portion // 2 <= TOPK:
                    rank(0, TT - HT, [portion // 2 - 1])

            def rank_end():
                done(ve.tensor_copy(small, tops[:, 0:TT]))
                ve.tensor_tensor(tops3, tops3, small.rearrange("p (o t) -> p o t", o=1).to_broadcast([P, TOPK, TT]),
                                 ALU.subtract).then_inc(s["rt_mask"], 1)
                done(ve.tensor_tensor(CAND, HOT[0], HOT[1], ALU.add))
                done(ve.tensor_tensor(CAND, CAND, HOT[2], ALU.add))
                ve.tensor_tensor(chosen, CAND, HOT[3], ALU.add).then_inc(s["rt_mask"], 1)

            def write_entries():
                ve.wait_ge(s["ramp"], 2)
                ve.wait_ge(s["rt_act"], 1)
                done(ve.reduce_sum(small, tops.rearrange("p (k t) -> p t k", k=TOPK), axis=AX.X))
                done(ve.reciprocal(small, small))
                done(ve.tensor_tensor(entry4[:, :, :, 1], tops.rearrange("p (k t) -> p t k", k=TOPK),
                                      small.rearrange("p (t o) -> p t o", o=1).to_broadcast([P, TT, TOPK]), ALU.mult))
                done(ve.tensor_copy(entry4[:, :, :, 2], rms[:, :].rearrange("p (t o) -> p t o", o=1).to_broadcast([P, TT, TOPK])))
                done(ve.memset(entry4[:, :, :, 3], 0.0))

            def count_before():
                ve.wait_ge(s["rt_pe"], 1)
                ve.tensor_copy(et(LG), ps_cnt[:, :].rearrange("p (t e) -> p e t", e=EXPERTS)).then_inc(s["cnt_copy"], 1)
                ve.wait_ge(s["cnt_copy"], 1)
                done(ve.tensor_tensor_scan(INCL, RESET, LG, 0.0, ALU.mult, ALU.add))
                done(ve.tensor_tensor(LG, INCL, LG, ALU.subtract))

            def set_bounds():
                counts = et(INCL)[:, :, TT - 1:TT].to_broadcast([P, EXPERTS, TT])
                done(ve.tensor_tensor(et(CAND), counts, ramp128.rearrange("p (o t) -> p o t", o=1).to_broadcast([P, EXPERTS, TT]),
                                      ALU.is_gt))
                done(ve.reduce_sum(small, et(CAND), axis=AX.X))
                done(ve.tensor_scalar(small, small, 1.0, None, ALU.max))
                done(ve.memset(rampf, 1.0))
                done(ve.tensor_tensor_scan(ends, rampf, small, 0.0, ALU.mult, ALU.add))
                done(ve.tensor_tensor(small, ends, small, ALU.subtract))
                done(ve.tensor_scalar(small, small, float(P), None, ALU.mult))
                done(ve.memset(bounds[:, 0:1], 0))
                done(ve.tensor_copy(bounds[:, 1:EXPERTS + 1], ends))
                done(ve.tensor_scalar(ends, ends, -1.0, None, ALU.add))
                done(ve.tensor_copy(finals[:, :], ends))

            def place_start():
                ve.wait_ge(s["rt_pe"], 2)
                done(ve.tensor_tensor(te(CAND), te(ps_cnt[:, :]), by_te(LG), ALU.add))
                done(ve.tensor_tensor(te(CAND), te(CAND), per_e(small), ALU.add))

            def place_choice(k):
                done(ve.tensor_tensor(INCL, HOT[k], CAND, ALU.mult))
                done(ve.reduce_sum(small, te(INCL), axis=AX.X))
                done(ve.tensor_copy(where.rearrange("p (t k) -> p t k", k=TOPK)[:, :, k], small))
                if k == TOPK - 1:
                    ve.memset(small, 0.0).then_inc(s["entry_ready"], 1)

            def route():
                ve.wait_ge(s["l_acc"], HALVES)
                rank(TT - HT, TT, list(range(TOPK)))
                rank_end()
                write_entries()
                count_before()
                set_bounds()
                place_start()
                for k in range(TOPK):
                    place_choice(k)

            def await_product(h, k):
                ve.wait_ge(s["product"], h * STEPS + (k + 1))

            def gate_scaled(h, j):
                k = CB + 2 * j
                await_product(h, k)
                wait(ve, "read_out", h * STEPS + (CB + 2 * j))
                ve.tensor_tensor(T, bank(k % 4), R, ALU.mult).then_inc(s["read_out"], 1)

            def gated_up(h, j):
                k = CB + 2 * j + 1
                await_product(h, k)
                ve.wait_ge(s["g_silu"], h * CB + (j + 1))
                wait(ve, "a_lo_s", h * CB + j)
                if j == 0:
                    ve.wait_ge(s["o_tr"], h * CB + 1)
                ve.tensor_tensor(OV, bank(k % 4), T, ALU.mult).then_inc(s["read_out"], 1)

            def down(h, o, k, hk):
                await_product(hk, k)
                if o == 0:
                    ve.wait_ge(s["a_lo_s"], (h + 1) * CB)
                ve.wait_ge(s["o_tr"], h * CB + (o + 1))
                ve.wait_ge(s["res"], h * CB + (o + 1))
                ve.tensor_tensor(OV, bank(k % 4), RES[:, o * HALF:(o + 1) * HALF], ALU.add).then_inc(s["read_out"], 1)

            def fill(h, i, first, prev, next_):
                if prev and i == 0:
                    gate_scaled(h - 1, CB - 1)
                if prev and i == 1:
                    gated_up(h - 1, CB - 1)
                if before_all(h):
                    return
                for o in range(CB):
                    if i == step_l(o) + 2:
                        ve.wait_ge(s["sig1"], h * CB + (o + 1))
                        ve.wait_ge(s["rl_in"], (h * CB + (o + 1)) * 16)
                        ve.tensor_tensor(C1[o % 2], C1[o % 2], RL, ALU.mult).then_inc(s["c1"], 1)
                        ve.wait_ge(s["c1"], h * CB + (o + 1))
                        wait(ve, "z_tr", h * CB + o)
                        wait(ve, "sums", h * CB + o)
                        wait(ve, "z_lo", h * CB + o)
                        if o == 0:
                            wait(ve, "l_tr", h)
                        ve.tensor_scalar(Z, C1[o % 2], nrm[:, o:o + 1], None, ALU.mult).then_inc(s["z"], 1)
                    if prev and i == step_d(o) + 1:
                        down(h - 1, o, number(step_d(o), False), h)
                    if i == step_l(o) + 1:
                        k = number(step_l(o), first)
                        await_product(h, k)
                        ve.wait_ge(xl_sem[o % 2], (h * (CB // 2) + (o // 2 + 1)) * 16)
                        ve.scalar_tensor_tensor(XL[o % 2], bank(k % 4), lsb[:, o:o + 1], XL[o % 2], ALU.mult, ALU.add)\
                            .then_inc(s["read_out"], 1)
                for o in range(CB):
                    part = slice(o * HALF, (o + 1) * HALF)
                    if i == step_d(o) + 1:
                        if prev:
                            ve.wait_ge(s["read_out"], summed(h - 1, o))
                        ve.wait_ge(s["c1"], h * CB + (o + 1))
                        ve.scalar_tensor_tensor(RES[:, part], XL[o % 2], lsb[:, CB + o:CB + o + 1], C1[o % 2],
                                                ALU.add, ALU.add).then_inc(s["res"], 1)
                if i == 2 * CB:
                    ve.wait_ge(s["sums"], h * CB + CB)
                    ve.tensor_scalar(SQ, SUM_BANK, 1.0 / CH, 1e-6, ALU.mult, ALU.add).then_inc(s["mean"], 1)
                if i == 2 * CB + 1:
                    ve.wait_ge(s["r_exp"], h + 1)
                    ve.wait_ge(s["mean"], h + 1)
                    wait(ve, "g_silu", h * CB)
                    steps = h * 3
                    ve.tensor_tensor(SG, R, R, ALU.mult).then_inc(s["newton_r"], 1)
                    ve.wait_ge(s["newton_r"], steps + 1)
                    ve.tensor_tensor(SG, SG, SQ, ALU.mult).then_inc(s["newton_r"], 1)
                    ve.wait_ge(s["newton_r"], steps + 2)
                    ve.tensor_scalar(SG, SG, -0.5, 1.5, ALU.mult, ALU.add).then_inc(s["newton_r"], 1)
                    ve.wait_ge(s["newton_r"], steps + 3)
                    ve.tensor_tensor(R, R, SG, ALU.mult).then_inc(s["r_set"], 1)
                    ve.wait_ge(s["r_set"], h + 1)
                    ve.wait_ge(s["z_lo"], h * CB + CB)
                    ve.tensor_tensor(Z[0:EXPERTS, :], LOGIT_BANK[0:EXPERTS, :], R[0:EXPERTS, :], ALU.mult).then_inc(s["scaled"], 1)
                    ve.tensor_copy(Z[EXPERTS:EXPERTS + 1, :], R[EXPERTS:EXPERTS + 1, :]).then_inc(s["scaled"], 1)
                if i == 2 * CB + 4:
                    ve.wait_ge(s["l_tr"], h + 1)
                    ve.tensor_copy(acc[:, ds(h * (HT * 33), HT * 33)].rearrange("p (t e) -> p t e", t=HT),
                                   Z_BANK.rearrange("p (t e) -> p t e", t=HT)[:, :, 0:33]).then_inc(s["l_acc"], 1)
                for j in range(CB - 1):
                    if i == step_g(j) + 2:
                        gate_scaled(h, j)
                    if i == step_g(j) + 3:
                        gated_up(h, j)
                if final(h, HALVES - 2) and i == 0:
                    ve.wait_ge(s["ek"], BLOCKS + 1)
                    ve.wait_ge(s["x_in"], 16 * (BLOCKS + 1))
                    ve.memset(K, 0.0).then_inc(s["zero_set"], 1)
                if final(h) and i > FIRST_RANK:
                    low_halves(ve, h, i, first, prev, next_)
                if final(h) and i == FIRST_RANK:
                    route()
                if final(h, HALVES - 2) and i >= FIRST_RANK:
                    rank_early(i - FIRST_RANK)

            def tail():
                gate_scaled(HALVES - 1, CB - 1)
                gate_r(ve, HALVES - 1, CB - 1)
                gate_silu(ve, HALVES - 1, CB - 1)
                gated_up(HALVES - 1, CB - 1)
                split_act_lo(ve, HALVES - 1, CB - 1)
                for o in range(CB):
                    if o + 1 < CB:
                        split_piece_lo(ve, HALVES, o + 1 - CB)
                    down(HALVES - 1, o, o - CB, HALVES)

            ve.wait_ge(s["masks"], 6)
            clip(0)
            with_halves(ve, unit, fill, tail)

            def split_x(g):
                ve.wait_ge(s["x_hi"], g + 1)
                ve.tensor_tensor(xlo, ps_xt[:, :], xhi.bitcast(f32), ALU.subtract).then_inc(s["x_lo"], 1)

            def split_weights(j, q):
                ve.wait_ge(s["w_hi"], j * GROUPS + q + 1)
                ve.tensor_tensor(wlo[:, q * GC:(q + 1) * GC], stage[:, q * GC:(q + 1) * GC],
                                 whi[:, q * GC:(q + 1) * GC].bitcast(f32), ALU.subtract).then_inc(s["w_lo"], 1)

            def gate_up(g, a):
                ve.wait_ge(s["silu_done"], g * 2 + a + 1)
                part = act[:, a * 256:a * 256 + 256]
                ve.scalar_tensor_tensor(part, ps_h[:, a * 512 + 256:a * 512 + 512], gains[:, ds(g + GT, 1)], part,
                                        ALU.mult, ALU.mult).then_inc(s["act_done"], 1)

            def split_act(g, a):
                ve.wait_ge(s["a_hi"], g * 2 + a + 1)
                ve.tensor_tensor(alo[:, a * 256:a * 256 + 256], ps_at[a], ahi[:, a * 256:a * 256 + 256].bitcast(f32),
                                 ALU.subtract).then_inc(s["a_lo"], 1)

            def weigh(g):
                ve.wait_ge(s["w2_read"], g * 2 + 3)
                ve.wait_ge(s["y_out"], (g + 1) * 16)
                ve.tensor_scalar(y[:, 512:1024], ps_y[:, 512:1024], gains[:, ds(g, 1)], None, ALU.mult).then_inc(s["y_lo"], 1)

            def tile(g, j):
                gate_up(g, 0)
                gate_up(g, 1)
                split_act(g, 0)
                split_act(g, 1)
                split_x(g + 1)
                weigh(g)

            def last_tile(g, j):
                gate_up(g, 0)
                split_weights(j + 1, 0)
                split_weights(j + 1, 1)
                gate_up(g, 1)
                split_act(g, 0)
                split_act(g, 1)
                split_x(g + 1)
                split_weights(j + 1, 2)
                split_weights(j + 1, 3)
                weigh(g)
                split_weights(j + 1, 4)
                split_weights(j + 1, 5)

            for q in range(GROUPS):
                split_weights(0, q)

            ve.wait_ge(s["slots_in"], 16)
            slots3 = slots.bitcast(f32).rearrange("p (t w) -> p t w", w=4)
            ve.tensor_copy(gains[:, 0:GT], slots3[:, :, 1]).then_inc(s["gains_set"], 1)
            ve.tensor_copy(gains[:, GT:2 * GT], slots3[:, :, 2]).then_inc(s["gains_set"], 1)
            split_x(0)
            expert_loop(ve, tile, last_tile)

        @block.tensor
        def _(pe):
            pe.wait_ge(s["masks"], 6)
            pe.wait_ge(s["consts_in"], 64)

            def product(h, k, hi, lo, ready, at):
                pe.wait_ge(s["piece_lo"], h * STEPS + (k + 1))
                wait(pe, "read_out", h * STEPS + (k - 3))
                for c in range(CB):
                    if ready:
                        pe.wait_ge(s[ready], at + (c + 1))
                    part = slice(c * HALF, (c + 1) * HALF)
                    for w, op in ((piece_hi, hi), (piece_hi, lo), (piece_lo, hi)):
                        last = pe.matmul(bank(k % 4), w[k % 2][:, c * P:(c + 1) * P], op[:, part],
                                         start=(c == 0 and w is piece_hi and op is hi), stop=(c == CB - 1 and w is piece_lo))
                last.then_inc(s["product"], 1)

            def by_token(h, o):
                pe.wait_ge(s["z"], h * CB + (o + 1))
                wait(pe, "z_copy", h * CB + o)
                if o == 0:
                    wait(pe, "l_acc", h)
                for t in range(HT):
                    last = pe.transpose(Z_BANK[:, t * P:(t + 1) * P], Z[:, t * P:(t + 1) * P], ident[:, :])
                last.then_inc(s["z_tr"], 1)
                if o == 0:
                    wait(pe, "scaled", h * 2)
                    wait(pe, "mean", h)
                pe.matmul(LOGIT_BANK[0:EXPERTS, :], rw[:, o * EXPERTS:(o + 1) * EXPERTS], Z, start=(o == 0), stop=(o == CB - 1))
                pe.wait_ge(s["sq"], h * CB + (o + 1))
                pe.matmul(SUM_BANK, ones[:, :], SQ, start=(o == 0), stop=(o == CB - 1)).then_inc(s["sums"], 1)

            def logits_by_token(h):
                pe.wait_ge(s["scaled"], h * 2 + 2)
                pe.wait_ge(s["z_copy"], h * CB + CB)
                for t in range(HT):
                    last = pe.transpose(Z_BANK[:, t * P:(t + 1) * P], Z[:, t * P:(t + 1) * P], ident[:, :])
                last.then_inc(s["l_tr"], 1)

            def out_by_token(h, o):
                pe.wait_ge(s["read_out"], summed(h, o))
                pe.wait_ge(s["o_copy"], h * CB + (o + 1))
                for t in range(HT):
                    last = pe.transpose(OUT_BANK[:, t * P:(t + 1) * P], OV[:, t * P:(t + 1) * P], ident[:, :])
                last.then_inc(s["o_tr"], 1)

            def count_chosen(before_each):
                if before_each:
                    pe.wait_ge(s["cnt_copy"], 1)
                else:
                    pe.wait_ge(s["rt_mask"], 2)
                for h in range(2):
                    last = pe.matmul(ps_cnt[:, h * 512:h * 512 + 512], (before if before_each else allb)[:, :],
                                     chosen[:, h * 512:h * 512 + 512], start=True, stop=True)
                last.then_inc(s["rt_pe"], 1)

            def half(h, first):
                ks = dict(products(h, first))
                for i in range(STEPS):
                    if i in ks:
                        if i >= 2 * CB:
                            product(h, ks[i], zhi, zlo, "z_lo" if i == 2 * CB else None, h * CB)
                        elif i in L_AT:
                            product(h, ks[i], chi, clo, "c_lo" if i == 0 else None, h * CB)
                        else:
                            product(h, ks[i], ahi_s, alo_s, "a_lo_s" if D_AT[i] == 0 else None, (h - 1) * CB)
                    for o in range(CB):
                        if i == step_l(o) + 2:
                            by_token(h, o)
                        if not first and i == step_d(o) + 1:
                            out_by_token(h - 1, o)
                    if i == 2 * CB + 2:
                        logits_by_token(h)
                    if final(h) and i == FIRST_RANK:
                        count_chosen(False)
                        count_chosen(True)

            half(0, True)
            with pe.Fori(1, HALVES - 1) as h:
                half(h, False)
            half(HALVES - 1, False)
            for o in range(CB):
                product(HALVES, o - CB, ahi_s, alo_s, "a_lo_s" if o == 0 else None, (HALVES - 1) * CB)
                if o:
                    out_by_token(HALVES - 1, o - 1)
            out_by_token(HALVES - 1, CB - 1)

            def transpose_x(g):
                pe.wait_ge(s["rows_in"], (g + 1) * 16)
                pe.wait_ge(s["x_lo"], g + 1)
                for c in range(CB):
                    last = pe.transpose(ps_xt[:, c * P:(c + 1) * P], hx[:, c * P:(c + 1) * P], ident[:, :])
                last.then_inc(s["x_tr"], 1)

            def transpose_act(g, a):
                pe.wait_ge(s["act_done"], g * 2 + a + 2)
                for i in range(2):
                    at = a * 256 + i * P
                    last = pe.transpose(ps_at[a][:, i * P:(i + 1) * P], act[:, at:at + P], ident[:, :])
                last.then_inc(s["a_tr"], 1)

            def tile(g, j):
                pe.wait_ge(s["x_lo"], g + 2)
                pe.wait_ge(s["act_done"], g * 2 + 1)
                for q in range(4):
                    a, kh = q // 2, q % 2
                    pe.wait_ge(s["w_lo"], j * GROUPS + q + 2)
                    for k in range(4):
                        xk = kh * 4 + k
                        rhs = slice(q * GC + k * 512, q * GC + k * 512 + 512)
                        for xp, wp in ((xhi, whi), (xhi, wlo), (xlo, whi)):
                            last = pe.matmul(ps_h[:, a * 512:a * 512 + 512], xp[:, xk * P:(xk + 1) * P], wp[:, rhs],
                                             start=(xk == 0 and xp is xhi and wp is whi), stop=(xk == 7 and xp is xlo))
                    last.then_inc(s["w1_read"], 1)
                transpose_act(g, 0)
                transpose_x(g + 1)
                transpose_act(g, 1)
                pe.wait_ge(s["y_lo"], g + 1)
                pe.wait_ge(s["y_hi"], g + 1)
                for q in range(2):
                    pe.wait_ge(s["w_lo"], j * GROUPS + q + 5 + 1)
                    pe.wait_ge(s["a_lo"], g * 2 + q + 1)
                    for k in range(2):
                        for ap_, wp in ((ahi, whi), (ahi, wlo), (alo, whi)):
                            for h in range(2):
                                rhs = (4 + q) * GC + k * 1024 + h * 512
                                last = pe.matmul(ps_y[:, h * 512:h * 512 + 512], ap_[:, (q * 2 + k) * P:(q * 2 + k + 1) * P],
                                                 wp[:, rhs:rhs + 512], start=(q == 0 and k == 0 and ap_ is ahi and wp is whi),
                                                 stop=(q == 1 and k == 1 and ap_ is alo))
                    last.then_inc(s["w2_read"], 1)

            transpose_x(0)
            expert_loop(pe, tile, tile)


def kernel(x, fside_BxSxS_0, cond_512, L0_cond_w, L0_cond_u, L0_ffn_weight, L0_ffn_scale_weight, L0_ffn_bias,
           L1_cond_w, L1_cond_u, L1_ffn_norm_w, L1_ffn_router_w, L1_ffn_w1, L1_ffn_w2, L1_ffn_sg, L1_ffn_su, L1_ffn_sd):
    import numpy as np
    import concourse.bacc as bacc
    from concourse.bass_utils import run_bass_kernel_spmd

    a = lambda v: np.asarray(v)
    by_partition = lambda v: a(v).reshape(CB, P).T
    blocks = lambda v: np.ascontiguousarray(a(v).transpose(0, 2, 1)).reshape(BLOCKS * P, SEQ)
    w1 = a(L1_ffn_w1).reshape(-1, 2, 4, P, 2, 2, 256).transpose(0, 5, 1, 3, 2, 4, 6).reshape(-1, 4, P, GC)
    w2 = a(L1_ffn_w2).reshape(-1, 2, 2, P, CH).transpose(0, 1, 3, 2, 4).reshape(-1, 2, P, GC)
    pieces = lambda v: v.reshape(CB, P, CB, P).transpose(2, 1, 0, 3).reshape(CB, P, PIECE)
    lin, gate, up, down = pieces(a(L0_ffn_weight).T), pieces(a(L1_ffn_sg)), pieces(a(L1_ffn_su)), pieces(a(L1_ffn_sd))
    steps = {}
    for o in range(CB):
        steps[step_l(o)], steps[step_d(o)], steps[step_g(o)], steps[step_g(o) + 1] = lin[o], down[o], gate[o], up[o]
    shared_w = np.stack([steps[i] for i in range(STEPS)]).reshape(STEPS * P, PIECE)
    expert_w = np.concatenate([w1, w2], 1).reshape(-1, GC)
    arrays = {
        "x_t": blocks(x),
        "side_t": blocks(fside_BxSxS_0),
        "cond": a(cond_512).reshape(1, -1),
        "w_all": np.concatenate([by_partition(L0_cond_w), by_partition(L1_cond_w)], 1),
        "u_all": np.concatenate([np.tile(by_partition(u), (1, BATCH)) for u in (L0_cond_u, L1_cond_u)], 1),
        "lin_sb": np.concatenate([by_partition(L0_ffn_scale_weight), by_partition(L0_ffn_bias)], 1),
        "norm_w": by_partition(L1_ffn_norm_w),
        "router_t": a(L1_ffn_router_w).reshape(EXPERTS, CB, P).transpose(2, 1, 0).reshape(P, CB * EXPERTS),
        "shared_w": shared_w,
        "expert_w": expert_w,
    }
    arrays = {k: np.ascontiguousarray(v) for k, v in arrays.items()}
    nc = bacc.Bacc("TRN2", target_bir_lowering=False, num_devices=1)
    ins = [nc.dram_tensor(k, v.shape, mybir.dt.from_np(v.dtype), kind="ExternalInput").ap() for k, v in arrays.items()]
    out = nc.dram_tensor("out", (TOK + P, CH), mybir.dt.float32, kind="ExternalOutput").ap()
    adaln_moe(nc, *ins, out)
    r = run_bass_kernel_spmd(nc, [arrays], core_ids=[0])
    return r.results[0]["out"][:TOK].reshape(BATCH, SEQ, CH)
```
